# Optimizing a Trainium2 kernel written in Bass

```python
import numpy as np
import jax
import jax.numpy as jnp

def _softmax(x, axis=-1):
    return jax.nn.softmax(x, axis=axis)

def _gelu(x):
    return jax.nn.gelu(x, approximate=True)

def _silu(x):
    return jax.nn.silu(x)

def _sigmoid(x):
    return jax.nn.sigmoid(x)

def _layernorm(x, axis=-1, eps=1e-05):
    m = jnp.mean(x, axis=axis, keepdims=True)
    v = jnp.var(x, axis=axis, keepdims=True)
    return (x - m) / jnp.sqrt(v + eps)

def _scatter_add(tgt, idx, src, axis=0):
    return tgt.at[idx].add(src)

def _segment_sum(src, seg, n):
    return jax.ops.segment_sum(src, seg, n)
kernel_name = 'mk_adj_resnorm_d2_adj_r2_8b7bb7'

def setup_inputs(seed: int=0):
    np.random.seed(seed)
    _w = jnp.asarray

    def _rec_inputs():
        import jax
        import jax.numpy as jnp
        _gk = jax.random.key(seed)
        x = -0.0005207 + 1.001 * jax.random.normal(jax.random.fold_in(_gk, 1), (4096, 128), jnp.float32)
        _w = (1.0 + jnp.arange(4096, dtype=jnp.float32)) ** (-0.5)
        _w = _w / _w.mean()
        _pij = jnp.clip(0.00195312 * _w[:, None] * _w[None, :], 0.0, 1.0)
        _a = jax.random.uniform(jax.random.fold_in(_gk, 2), (4096, 4096)) < _pij
        _a = jnp.logical_or(_a, jnp.eye(4096, dtype=bool))
        _af = _a.astype(jnp.float32)
        _af = _af * jax.random.uniform(jax.random.fold_in(_gk, 3), (4096, 4096), jnp.float32, 0.05, 1)
        adj = _af
        return (x, adj)
    x, adj = _rec_inputs()

    def _L0_gnn_setup():
        import jax, jax.numpy as jnp
        import numpy as np
        N = 4096
        D = 128
        L = 3

        def _cxin_conv(x, a, eps, W, b):
            ax = a @ x
            h = ax + (1.0 + eps[0]) * ax
            for i in range(L):
                h = jax.nn.relu(h @ W[i].T + b[i])
            return h
        key = jax.random.key(seed)
        ks = jax.random.split(key, 8)
        s = 1.0 / np.sqrt(D)
        return {'x1': jax.random.normal(ks[0], (N, D), jnp.float32), 'x2': jax.random.normal(ks[1], (N, D), jnp.float32), 'G1': jax.random.uniform(ks[2], (N, N), jnp.float32), 'G2': jax.random.uniform(ks[3], (N, N), jnp.float32), 'eps1': jnp.zeros((1,), jnp.float32), 'eps2': jnp.zeros((1,), jnp.float32), 'W1': jax.random.normal(ks[4], (L, D, D), jnp.float32) * s, 'b1': jnp.zeros((L, D), jnp.float32), 'W2': jax.random.normal(ks[5], (L, D, D), jnp.float32) * s, 'b2': jnp.zeros((L, D), jnp.float32), 'Wm': jax.random.normal(ks[6], (D, 2 * D), jnp.float32) * (1.0 / np.sqrt(2 * D)), 'bm': jnp.zeros((D,), jnp.float32)}
    _L0_gnn_all = _L0_gnn_setup()
    _L0_gnn_in = {k: v for k, v in _L0_gnn_all.items() if k in ('x2', 'eps1', 'eps2', 'W1', 'b1', 'W2', 'b2', 'Wm', 'bm')}
    del _L0_gnn_all

    def _L1_gnn_setup():
        import jax, jax.numpy as jnp
        import numpy as np
        THRESH = 1e-06
        EPS = 1e-08
        LN_EPS = 1e-05

        def _layer(h, M, W_in, b_in, W_out, b_out, W_self, b_self, gamma, beta):
            A = M / (jnp.sum(M, axis=0, keepdims=True) + EPS)
            mask = A > THRESH
            W = jnp.where(mask, A, 0.0)
            T = h @ W_in + b_in
            weighted_sum = jnp.einsum('ji,jd->id', W, T)
            weight_sum = jnp.sum(W, axis=0)
            has_edge = jnp.any(mask, axis=0)
            agg = jnp.where(has_edge[:, None], weighted_sum / (weight_sum[:, None] + EPS), T)
            agg = agg @ W_out + b_out
            out = agg + (h @ W_self + b_self)
            mu = jnp.mean(out, axis=-1, keepdims=True)
            var = jnp.mean(jnp.square(out - mu), axis=-1, keepdims=True)
            out = (out - mu) * jax.lax.rsqrt(var + LN_EPS) * gamma + beta
            return out
        key = jax.random.key(seed)
        ks = jax.random.split(key, 16)
        N, D_IN, D_H, D_OUT = (4096, 128, 256, 128)
        s = 0.05
        return {'node_features': jax.random.normal(ks[0], (N, D_IN), jnp.float32), 'mobility_matrix': jax.random.uniform(ks[1], (N, N), jnp.float32), 'W_in1': jax.random.normal(ks[2], (D_IN, D_H)) * s, 'b_in1': jnp.zeros((D_H,)), 'W_out1': jax.random.normal(ks[3], (D_H, D_H)) * s, 'b_out1': jnp.zeros((D_H,)), 'W_self1': jax.random.normal(ks[4], (D_IN, D_H)) * s, 'b_self1': jnp.zeros((D_H,)), 'g1': jnp.ones((D_H,)), 'be1': jnp.zeros((D_H,)), 'W_in2': jax.random.normal(ks[5], (D_H, D_OUT)) * s, 'b_in2': jnp.zeros((D_OUT,)), 'W_out2': jax.random.normal(ks[6], (D_OUT, D_OUT)) * s, 'b_out2': jnp.zeros((D_OUT,)), 'W_self2': jax.random.normal(ks[7], (D_H, D_OUT)) * s, 'b_self2': jnp.zeros((D_OUT,)), 'g2': jnp.ones((D_OUT,)), 'be2': jnp.zeros((D_OUT,))}
    _L1_gnn_all = _L1_gnn_setup()
    _L1_gnn_in = {k: v for k, v in _L1_gnn_all.items() if k in ('W_in1', 'b_in1', 'W_out1', 'b_out1', 'W_self1', 'b_self1', 'g1', 'be1', 'W_in2', 'b_in2', 'W_out2', 'b_out2', 'W_self2', 'b_self2', 'g2', 'be2')}
    del _L1_gnn_all
    return {'x': x, 'adj': adj, 'L0_gnn_x2': _L0_gnn_in['x2'], 'L0_gnn_eps1': _L0_gnn_in['eps1'], 'L0_gnn_eps2': _L0_gnn_in['eps2'], 'L0_gnn_W1': _L0_gnn_in['W1'], 'L0_gnn_b1': _L0_gnn_in['b1'], 'L0_gnn_W2': _L0_gnn_in['W2'], 'L0_gnn_b2': _L0_gnn_in['b2'], 'L0_gnn_Wm': _L0_gnn_in['Wm'], 'L0_gnn_bm': _L0_gnn_in['bm'], 'L1_gnn_W_in1': _L1_gnn_in['W_in1'], 'L1_gnn_b_in1': _L1_gnn_in['b_in1'], 'L1_gnn_W_out1': _L1_gnn_in['W_out1'], 'L1_gnn_b_out1': _L1_gnn_in['b_out1'], 'L1_gnn_W_self1': _L1_gnn_in['W_self1'], 'L1_gnn_b_self1': _L1_gnn_in['b_self1'], 'L1_gnn_g1': _L1_gnn_in['g1'], 'L1_gnn_be1': _L1_gnn_in['be1'], 'L1_gnn_W_in2': _L1_gnn_in['W_in2'], 'L1_gnn_b_in2': _L1_gnn_in['b_in2'], 'L1_gnn_W_out2': _L1_gnn_in['W_out2'], 'L1_gnn_b_out2': _L1_gnn_in['b_out2'], 'L1_gnn_W_self2': _L1_gnn_in['W_self2'], 'L1_gnn_b_self2': _L1_gnn_in['b_self2'], 'L1_gnn_g2': _L1_gnn_in['g2'], 'L1_gnn_be2': _L1_gnn_in['be2']}

def reference(x, adj, L0_gnn_x2, L0_gnn_eps1, L0_gnn_eps2, L0_gnn_W1, L0_gnn_b1, L0_gnn_W2, L0_gnn_b2, L0_gnn_Wm, L0_gnn_bm, L1_gnn_W_in1, L1_gnn_b_in1, L1_gnn_W_out1, L1_gnn_b_out1, L1_gnn_W_self1, L1_gnn_b_self1, L1_gnn_g1, L1_gnn_be1, L1_gnn_W_in2, L1_gnn_b_in2, L1_gnn_W_out2, L1_gnn_b_out2, L1_gnn_W_self2, L1_gnn_b_self2, L1_gnn_g2, L1_gnn_be2):
    import jax
    import jax.numpy as jnp

    def _L0_gnn_ref(x1, x2, G1, G2, eps1, eps2, W1, b1, W2, b2, Wm, bm):
        import jax, jax.numpy as jnp
        import numpy as np
        N = 4096
        D = 128
        L = 3

        def _cxin_conv(x, a, eps, W, b):
            ax = a @ x
            h = ax + (1.0 + eps[0]) * ax
            for i in range(L):
                h = jax.nn.relu(h @ W[i].T + b[i])
            return h
        out1 = _cxin_conv(x1, G1, eps1, W1, b1)
        out2 = _cxin_conv(x2, G2, eps2, W2, b2)
        merged = jnp.concatenate((out1, out2), axis=1)
        return merged @ Wm.T + bm

    def _L1_gnn_ref(node_features, mobility_matrix, W_in1, b_in1, W_out1, b_out1, W_self1, b_self1, g1, be1, W_in2, b_in2, W_out2, b_out2, W_self2, b_self2, g2, be2):
        import jax, jax.numpy as jnp
        import numpy as np
        THRESH = 1e-06
        EPS = 1e-08
        LN_EPS = 1e-05

        def _layer(h, M, W_in, b_in, W_out, b_out, W_self, b_self, gamma, beta):
            A = M / (jnp.sum(M, axis=0, keepdims=True) + EPS)
            mask = A > THRESH
            W = jnp.where(mask, A, 0.0)
            T = h @ W_in + b_in
            weighted_sum = jnp.einsum('ji,jd->id', W, T)
            weight_sum = jnp.sum(W, axis=0)
            has_edge = jnp.any(mask, axis=0)
            agg = jnp.where(has_edge[:, None], weighted_sum / (weight_sum[:, None] + EPS), T)
            agg = agg @ W_out + b_out
            out = agg + (h @ W_self + b_self)
            mu = jnp.mean(out, axis=-1, keepdims=True)
            var = jnp.mean(jnp.square(out - mu), axis=-1, keepdims=True)
            out = (out - mu) * jax.lax.rsqrt(var + LN_EPS) * gamma + beta
            return out
        h = _layer(node_features, mobility_matrix, W_in1, b_in1, W_out1, b_out1, W_self1, b_self1, g1, be1)
        h = jax.nn.relu(h)
        h = _layer(h, mobility_matrix, W_in2, b_in2, W_out2, b_out2, W_self2, b_self2, g2, be2)
        h = jax.nn.relu(h)
        return h
    x = _layernorm(x + _L0_gnn_ref(x, L0_gnn_x2, adj, adj, L0_gnn_eps1, L0_gnn_eps2, L0_gnn_W1, L0_gnn_b1, L0_gnn_W2, L0_gnn_b2, L0_gnn_Wm, L0_gnn_bm), axis=-1)
    x = _layernorm(x + _L1_gnn_ref(x, adj, L1_gnn_W_in1, L1_gnn_b_in1, L1_gnn_W_out1, L1_gnn_b_out1, L1_gnn_W_self1, L1_gnn_b_self1, L1_gnn_g1, L1_gnn_be1, L1_gnn_W_in2, L1_gnn_b_in2, L1_gnn_W_out2, L1_gnn_b_out2, L1_gnn_W_self2, L1_gnn_b_self2, L1_gnn_g2, L1_gnn_be2), axis=-1)
    return x

_drawn_inputs = setup_inputs


def setup_inputs(seed=0):
    import zlib

    import numpy as np

    out = dict(_drawn_inputs(seed))
    spreads = {'L0_gnn_b1': (0.0, 0.1),
     'L0_gnn_b2': (0.0, 0.1),
     'L0_gnn_bm': (0.0, 0.1),
     'L1_gnn_b_in1': (0.0, 0.1),
     'L1_gnn_b_out1': (0.0, 0.1),
     'L1_gnn_b_self1': (0.0, 0.1),
     'L1_gnn_g1': (1.0, 0.2),
     'L1_gnn_be1': (0.0, 0.1),
     'L1_gnn_b_in2': (0.0, 0.1),
     'L1_gnn_b_out2': (0.0, 0.1),
     'L1_gnn_b_self2': (0.0, 0.1),
     'L1_gnn_g2': (1.0, 0.2),
     'L1_gnn_be2': (0.0, 0.1)}
    factors = {}
    for name, (base, spread) in spreads.items():
        noise = np.random.default_rng([zlib.crc32(name.encode()), seed]).standard_normal(out[name].shape)
        drawn = base * np.exp(spread * noise) if base else spread * noise
        out[name] = jnp.asarray(drawn.astype(out[name].dtype))
    for name, factor in factors.items():
        out[name] = (out[name] * factor).astype(out[name].dtype)
    return out
```

```python
import numpy as np
import concourse.bass as bass
from concourse import mybir
from contextlib import ExitStack

N = 4096
D = 128
DH = 256
LAYERS = 3
TN = N // D
CH = 512
NCH = N // CH
TPC = CH // D
KT = 2
G = TN // KT
XT = 2 * TN // 8
TILES = NCH * G
LOAD = KT * CH
NRAW = 8
NSPLIT = 4
LOOK = 2
THRESH = 1e-06
EPS = 1e-08
LN_EPS = 1e-05
SMALL = 2 * THRESH * N
SUM_LIMIT = 1.5 * N


def gnn_kernel(nc, adj_rows, adj_cols, x_in, x2_in, mlp_w, merge_w, win1_t, wout1, wself1,
               win2_t, wout2, wself2, cols_in, rows_in, eps_in, ident_in, r_dram, out):
    f32, f32r, i32 = mybir.dt.float32, mybir.dt.float32r, mybir.dt.int32
    ALU, ACT, AX = mybir.AluOpType, mybir.ActivationFunctionType, mybir.AxisListType
    ds = bass.ds
    ctx = ExitStack()
    with ctx:
        def sb(name, shape, dt=f32):
            return ctx.enter_context(nc.sbuf_tensor(name, shape, dt))

        def sem(name):
            return ctx.enter_context(nc.semaphore(name))

        raw = sb("raw", [128, NRAW, LOAD])
        hi = sb("hi", [128, NSPLIT, LOAD], f32r)
        lo = sb("lo", [128, NSPLIT, LOAD], f32r)
        xs_hi = sb("xs_hi", [128, 2, N], f32r)
        xs_lo = sb("xs_lo", [128, 2, N], f32r)
        h_hi = sb("h_hi", [128, N], f32r)
        h_lo = sb("h_lo", [128, N], f32r)
        t_hi, t_lo = xs_hi[:, 0, :], xs_lo[:, 0, :]
        own_hi, own_lo = xs_hi[:, 1, :], xs_lo[:, 1, :]

        mlp = sb("mlp", [128, 2 * LAYERS, D])
        merge = sb("merge", [128, 2, D])
        w_self1 = sb("w_self1", [128, DH])
        w_c1 = sb("w_c1", [128, DH])
        w_2 = sb("w_2", [128, 2, 2, D])
        w_in2t = sb("w_in2t", [128, 2, D])
        bias_cols = sb("bias_cols", [128, 13])
        bias_rows = sb("bias_rows", [128, 7 * D + 2 * DH])
        bm_row = bias_rows[:, 0:D]
        g2_row = bias_rows[:, D:2 * D]
        be2_row = bias_rows[:, 2 * D:3 * D]
        b_out2 = bias_rows[:, 3 * D:4 * D]
        b_self2 = bias_rows[:, 4 * D:5 * D]
        bc2_row = bias_rows[:, 5 * D:6 * D]
        b_out1 = bias_rows[:, 7 * D:7 * D + DH]
        b_self1 = bias_rows[:, 7 * D + DH:7 * D + 2 * DH]
        bc1_row = sb("bc1_row", [128, DH])
        col_rep = sb("col_rep", [128, 3, 128])
        scale = sb("scale", [128, 2])
        ident = sb("ident", [128, 128])
        ones = sb("ones", [128, 128])
        ln_eps = sb("ln_eps", [128, 1])

        wk = sb("wk", [128, 8, CH])
        axA, axB, m1A, m1B = wk[:, 0, :], wk[:, 1, :], wk[:, 2, :], wk[:, 3, :]
        res0, y0 = wk[:, 4, :], wk[:, 5, :]
        ut, u_n, u_t, h_t = wk[:, 0, :], wk[:, 1, :], wk[:, 2, :], wk[:, 3, :]
        h_n = wk[:, 4, :]
        y1 = wk[:, 5:7, :].rearrange("p a (b n) -> p (a b) n", b=2)
        wk_sum = wk[:, 7, :]
        h2t = sb("h2t", [128, 2, CH])
        z2 = h2t[:, 0, :]
        z3 = h2t[:, 1, :]
        stats = sb("stats", [128, TPC, 6])
        mv = sb("mv", [128, TPC, 2])
        std = sb("std", [128, TPC])
        rstd = sb("rstd", [128, TPC])
        nd = sb("nd", [128, 4, TPC])
        s_part = sb("s_part", [128, TN * NCH])
        small_n = sb("small_n", [128, TILES + 1])
        s_all = sb("s_all", [128, TN])
        r_all = sb("r_all", [128, TN])
        r_use = sb("r_use", [128, TN])
        ws_fast = sb("ws_fast", [128, TN])
        over = sb("over", [128, TN])
        bad = sb("bad", [128, 4])
        flag_i = sb("flag_i", [128, 1], i32)
        qe = sb("qe", [128, TN])
        ne = sb("ne", [128, TN])
        beta = sb("beta", [128, TN])
        r_rows = sb("r_rows", [TN, 128])
        rb = sb("rb", [128, 2 * CH])
        w_acc = sb("w_acc", [128, 2 * CH])

        big = ctx.enter_context(nc.psum_tensor("big", [128, 4 * CH], f32))
        sm = ctx.enter_context(nc.psum_tensor("sm", [128, 4, CH], f32))
        pair = big[:, 2 * CH:4 * CH].rearrange("p (t n) -> p t n", n=DH)

        raw_in = [sem(f"raw_in{s}") for s in range(NRAW)]
        w_in = sem("w_in")
        setup = sem("setup")
        prod_ps = sem("prod_ps")
        prod_sb = sem("prod_sb")
        masked = sem("masked")
        gen = sem("gen")
        hi_done = sem("hi_done")
        count_done = sem("count_done")
        lo_done = sem("lo_done")
        used = sem("used")
        agg_out = sem("agg_out")
        mlp_ps = sem("mlp_ps")
        mlp_sb = sem("mlp_sb")
        merged = sem("merged")
        v0 = sem("v0")
        v1 = sem("v1")
        v2 = sem("v2")
        var0 = sem("var0")
        std0 = sem("std0")
        h_nat = sem("h_nat")
        h_hi_done = sem("h_hi_done")
        h_lo_done = sem("h_lo_done")
        totals = sem("totals")
        flag_ps = sem("flag_ps")
        flag_v = sem("flag_v")
        r_rows_sb = sem("r_rows_sb")
        r_stored = sem("r_stored")
        rb_in = sem("rb_in")
        wsum_in = sem("wsum_in")
        wsum_ps = sem("wsum_ps")
        node_v = sem("node_v")
        u_ps = sem("u_ps")
        u_sb = sem("u_sb")
        ut_ps = sem("ut_ps")
        ut_sb = sem("ut_sb")
        hn_sb = sem("hn_sb")
        o1_ps = sem("o1_ps")
        var1 = sem("var1")
        std1 = sem("std1")
        z_sb = sem("z_sb")
        z_ps = sem("z_ps")
        h2_sb = sem("h2_sb")
        g2_ps = sem("g2_ps")
        g2_sb = sem("g2_sb")
        t_lo_done = sem("t_lo_done")
        t_ps = sem("t_ps")
        var2 = sem("var2")
        std2 = sem("std2")
        out_sb = sem("out_sb")
        passed = sem("passed")
        out_done = sem("out_done")

        class Chain:

            def __init__(self, eng, s, per_chunk, c):
                self.eng, self.sem, self.k, self.c, self.n = eng, s, per_chunk, c, 0

            def step(self, ins):
                self.n += 1
                ins.then_inc(self.sem, 1)

            def wait(self):
                wait_ge(self.eng, self.sem, self.c * self.k + self.n)

        def wait_ge(eng, s, value):
            assert not isinstance(value, int) or value > 0
            eng.wait_ge(s, value)

        V0, V1, V2 = 5, 12, 14

        def at(p, c, g):
            return XT + p * TILES + c * G + g

        def aggregated(eng, p, c):
            wait_ge(eng, used, c * G + (p * TILES + G))

        def uses(p, c, g):
            return XT // NRAW + (p * TILES + c * G + g) // NRAW + 1 if isinstance(c, int) \
                else c * (G // NRAW) + (XT // NRAW + (p * TILES + g) // NRAW + 1)

        def tile_of(mem, g, n, f=LOAD):
            return mem[:, g % n, 0:f]

        block = ctx.enter_context(nc.Block())

        def sweep(eng, body):
            body(0)
            with eng.Fori(1, NCH) as c:
                body(c)

        @block.sync
        def _(sp):
            for n in range(XT):
                src = (x_in, x2_in)[n % 2][:, (n // 2) * LOAD:(n // 2 + 1) * LOAD]
                sp.dma_start(raw[:, n, :], src).then_inc(raw_in[n], 16)
            for p in range(3):
                def loads(c, p=p):
                    for g in range(G):
                        wait_ge(sp, lo_done, at(p, c, g) - NRAW + 1)
                        src = (adj_rows if p == 0 else adj_cols)[ds(c * G + g, 1)]
                        sp.dma_start(raw[:, g % NRAW, :], src.rearrange("a p n -> p (a n)"))\
                          .then_inc(raw_in[g % NRAW], 16)
                sweep(sp, loads)

            sp.wait_ge(out_done, 16 * NCH + 16)

        @block.gpsimd
        def _(pool):
            pool.wait_ge(r_rows_sb, 1)
            pool.dma_start(r_dram, r_rows[:, :]).then_inc(r_stored, 16)
            pool.wait_ge(r_stored, 16)

            def load_row(n):
                src = r_dram[ds((n % NCH) * TPC, TPC), :].rearrange("t n -> (t n)")
                pool.dma_start(rb[:, ds((n % 2) * CH, CH)], src.partition_broadcast(128)).then_inc(rb_in, 16)
            load_row(0)
            pool.wait_ge(rb_in, 16)
            load_row(1)
            with pool.Fori(2, 2 * NCH) as n:
                wait_ge(pool, rb_in, n * 16)
                wait_ge(pool, lo_done, n * G + at(1, -1, 0))
                load_row(n)
            pool.wait_ge(rb_in, 16 * 2 * NCH)

        @block.scalar
        def _(act):
            for dst, src in ((mlp[:, :, :], mlp_w), (merge[:, :, :], merge_w), (w_self1[:, :], wself1),
                             (w_2[:, :, 1, :], wself2), (w_in2t[:, :, :], win2_t), (ident[:, :], ident_in),
                             (bias_cols[:, :], cols_in),
                             (bias_rows[:, :], rows_in.partition_broadcast(128)),
                             (scale[:, :], eps_in.partition_broadcast(128)),
                             (axA[:, 0:DH], win1_t), (m1A, wout1), (y0[:, 0:D], wout2)):
                act.dma_start(dst, src).then_inc(w_in, 16)

            for n in range(XT):
                act.wait_ge(raw_in[n], 16)
                nc.scalar.activation(xs_hi[:, n % 2, (n // 2) * LOAD:(n // 2 + 1) * LOAD], raw[:, n, :],
                                     ACT.Copy).then_inc(hi_done, 1)
            act.wait_ge(prod_ps, 1)
            nc.scalar.copy(w_c1[:, :], sm[:, 0, 0:DH])
            nc.scalar.copy(bc1_row[:, :], sm[:, 1, 0:DH])
            nc.scalar.copy(w_2[:, :, 0, :], sm[:, 2, 0:2 * D].rearrange("p (a n) -> p a n", a=2))
            nc.scalar.copy(bc2_row, sm[:, 3, 0:D]).then_inc(prod_sb, 1)

            def split(p, c, g):
                wait_ge(act, raw_in[g % NRAW], 16 * uses(p, c, g))
                if p:
                    wait_ge(act, masked, c * G + ((p - 1) * TILES + g + 1))
                if not (p == 0 and isinstance(c, int) and g < NSPLIT):
                    wait_ge(act, used, at(p, c, g) - XT - NSPLIT + 1)
                dst = hi[:, g % NSPLIT, :]
                src = raw[:, g % NRAW, :]
                if p:
                    nc.scalar.activation(dst, src, ACT.Copy).then_inc(hi_done, 1)
                    return
                for k in range(KT):
                    last = nc.scalar.activation(dst[:, k * CH:(k + 1) * CH], src[:, k * CH:(k + 1) * CH], ACT.Copy,
                                                accum_out=s_part[:, ds(c + (g * KT + k) * NCH, 1)])
                last.then_inc(hi_done, 1)

            def finish0(g, c):
                if g == 2:
                    aggregated(act, 0, c)
                    bank = (c % 2) * CH
                    nc.scalar.activation(axA, big[:, ds(bank, CH)], ACT.Copy, scale=scale[:, 0:1])
                    nc.scalar.activation(axB, big[:, ds(bank + 2 * CH, CH)], ACT.Copy,
                                         scale=scale[:, 1:2]).then_inc(agg_out, 1)
                if g in (4, 6, 8):
                    layer = (g - 4) // 2
                    wait_ge(act, mlp_ps, c * LAYERS + layer + 1)
                    dst = ((m1A, m1B), (axA, axB))[layer % 2]
                    for b in range(2):
                        last = nc.scalar.activation(dst[b], sm[:, b, :], ACT.Relu,
                                                    bias=bias_cols[:, b * LAYERS + layer:b * LAYERS + layer + 1])
                    last.then_inc(mlp_sb, 1)
                if g == 12:
                    wait_ge(act, var0, c + 1)
                    nc.scalar.activation(std[:, :], mv[:, :, 1], ACT.Sqrt, bias=ln_eps[:, :]).then_inc(std0, 1)
                if g == 13:
                    wait_ge(act, h_nat, c + 1)
                    nc.scalar.activation(h_hi[:, ds(c * CH, CH)], y0, ACT.Copy).then_inc(h_hi_done, 1)

            def finish1(g, c):
                if g == 2:
                    aggregated(act, 1, c)
                    nc.scalar.activation(ut, big[:, ds((c % 2) * CH, CH)], ACT.Copy).then_inc(agg_out, 1)
                if g == 5:
                    wait_ge(act, ut_ps, c + 1)
                    nc.scalar.activation(u_t, sm[:, 1, :], ACT.Copy)
                    nc.scalar.activation(h_t, sm[:, 2, :], ACT.Copy).then_inc(ut_sb, 1)
                if g == 10:
                    wait_ge(act, var1, c + 1)
                    nc.scalar.activation(std[:, :], mv[:, :, 1], ACT.Sqrt, bias=ln_eps[:, :]).then_inc(std1, 1)
                if g == 12:
                    wait_ge(act, z_ps, c + 1)
                    for b in range(2):
                        last = nc.scalar.activation(h2t[:, b, :], sm[:, b, :], ACT.Relu,
                                                    scale=bias_cols[:, 6 + b:7 + b], bias=bias_cols[:, 8 + b:9 + b])
                    last.then_inc(h2_sb, 1)
                if g == 14:
                    wait_ge(act, g2_ps, c + 1)
                    g2 = sm[:, 2:4, :].rearrange("p a (b m n) -> p (a b) m n", b=2, m=2)
                    nc.scalar.activation(t_hi[:, ds(c * CH, CH)].rearrange("p (t n) -> p t n", n=D),
                                         g2[:, :, 0, :], ACT.Copy)
                    nc.scalar.activation(own_hi[:, ds(c * CH, CH)].rearrange("p (t n) -> p t n", n=D),
                                         g2[:, :, 1, :], ACT.Copy).then_inc(g2_sb, 1)

            def finish2(g, c):
                if g == 2:
                    aggregated(act, 2, c)
                    nc.scalar.activation(ut, big[:, ds((c % 2) * CH, CH)], ACT.Copy).then_inc(agg_out, 1)
                if g in (7, 10):
                    k = (g - 7) // 3
                    wait_ge(act, var2, c * 2 + k + 1)
                    nc.scalar.activation(std[:, :], mv[:, :, 1], ACT.Sqrt, bias=ln_eps[:, :]).then_inc(std2, 1)

                if g == 13:
                    wait_ge(act, out_sb, c + 1)
                    act.dma_start(out[ds(c, 1)].rearrange("a p n -> p (a n)"), z3).then_inc(out_done, 16)

            finish = (finish0, finish1, finish2)
            act.wait_ge(setup, 1)
            for p in range(3):
                def chunk(c, p=p):
                    first = isinstance(c, int)
                    for g in range(G):
                        split(p, c, g)
                        if first and p:
                            finish[p - 1](g, NCH - 1)
                        elif not first:
                            finish[p](g, c - 1)
                sweep(act, chunk)
            for g in range(G):
                finish2(g, NCH - 1)

        @block.vector
        def _(dve):
            dve.sem_inc(out_done, 16)
            nc.vector.memset(ones[:, :], 1.0)
            nc.vector.memset(w_acc[:, :], 0.0)
            nc.vector.memset(ln_eps[:, :], LN_EPS)
            dve.wait_ge(w_in, 16 * 12)
            nc.vector.tensor_scalar(scale[:, :], scale[:, :], 1.0, 1.0, ALU.add, ALU.add)
            nc.vector.tensor_tensor(b_out1, b_out1, b_self1, ALU.add)
            nc.vector.tensor_tensor(b_out2, b_out2, b_self2, ALU.add)
            for b in range(3):
                last = nc.vector.tensor_scalar(col_rep[:, b, :], ident[:, :], 0.0, bias_cols[:, 10 + b:11 + b],
                                               ALU.mult, ALU.add)
            last.then_inc(setup, 1)
            dve.wait_ge(setup, 1)

            for n in range(XT):
                cols = slice((n // 2) * LOAD, (n // 2 + 1) * LOAD)
                dve.wait_ge(hi_done, n + 1)
                nc.vector.tensor_tensor(xs_lo[:, n % 2, cols], raw[:, n, :], xs_hi[:, n % 2, cols].bitcast(f32),
                                        ALU.subtract).then_inc(lo_done, 1)

            def split(p, c, g):
                first = p == 0 and isinstance(c, int)
                src, low = raw[:, g % NRAW, :], lo[:, g % NSPLIT, :]
                if p == 0:
                    wait_ge(dve, raw_in[g % NRAW], 16 * uses(p, c, g))
                    if not (first and g < NSPLIT):
                        wait_ge(dve, used, at(p, c, g) - XT - NSPLIT + 1)
                    nc.vector.scalar_tensor_tensor(low, src, SMALL, src, ALU.is_le, ALU.logical_and,
                                                   accum_out=small_n[:, ds(c * G + g, 1)]).then_inc(count_done, 1)
                    wait_ge(dve, count_done, c * G + g + 1)
                wait_ge(dve, hi_done, at(p, c, g) + 1)
                nc.vector.tensor_tensor(low, src, hi[:, g % NSPLIT, :].bitcast(f32), ALU.subtract)\
                    .then_inc(lo_done, 1)

            def mask(p, c, g, flag):
                n = c * G + ((p - 1) * TILES + g)
                src = raw[:, g % NRAW, :]
                with dve.If(flag == 1):
                    before = n * 3 if p == 1 else n + 2 * TILES
                    half = (c % 2) * CH
                    wait_ge(dve, rb_in, (c + ((p - 1) * NCH + 1)) * 16)
                    wait_ge(dve, raw_in[g % NRAW], 16 * uses(p, c, g))
                    for k in range(KT):
                        part = src[:, k * CH:(k + 1) * CH]
                        last = nc.vector.tensor_tensor(part, part, rb[:, ds(half, CH)], ALU.mult)
                    last.then_inc(gen, 1)
                    wait_ge(dve, gen, before + 1)
                    made = nc.vector.scalar_tensor_tensor(src, src, THRESH, src, ALU.is_gt, ALU.mult)
                    if p == 2:
                        made.then_inc(masked, 1)
                    else:
                        made.then_inc(gen, 1)
                        wait_ge(dve, gen, before + 2)
                        acc = w_acc[:, ds(half, CH)]
                        parts = [src[:, k * CH:(k + 1) * CH] for k in range(KT)]
                        if g == 0:
                            if not (isinstance(c, int) and c < 2):
                                wait_ge(dve, wsum_in, c - 1)
                            nc.vector.tensor_copy(acc, parts[0]).then_inc(gen, 1)
                        else:
                            wait_ge(dve, masked, n)
                            nc.vector.tensor_tensor(acc, acc, parts[0], ALU.add).then_inc(gen, 1)
                        wait_ge(dve, gen, before + 3)
                        nc.vector.tensor_tensor(acc, acc, parts[1], ALU.add).then_inc(masked, 1)
                with dve.Else():
                    dve.sem_inc(masked, 1)

            def layer_norm_stats(chain, y, width, ready):
                chain.wait()
                for t in range(TPC):
                    last = nc.vector.bn_stats(stats[:, t, :], y[:, t * width:(t + 1) * width])
                chain.step(last)
                chain.wait()
                dve.sem_inc(passed, 1)
                for t in range(TPC):
                    last = nc.vector.bn_aggr(mv[:, t, :], stats[:, t, :])
                last.then_inc(ready, 1)

            def normalise(chain, dst, y, width):
                chain.step(nc.vector.reciprocal(rstd[:, :], std[:, :]))
                chain.wait()
                for t in range(TPC):
                    cols = slice(t * width, (t + 1) * width)
                    last = nc.vector.tensor_scalar(dst[:, cols], y[:, cols], mv[:, t, 0:1], rstd[:, t:t + 1],
                                                   ALU.subtract, ALU.mult)
                return last

            chains = {}

            def row4(row):
                return row.rearrange("p (a n) -> p a n", a=1).broadcast_to([128, TPC, row.shape[-1]])

            def t4(x):
                return x.rearrange("p (t n) -> p t n", t=TPC)

            def finish0(g, c):
                if g == 6:
                    k = chains[0] = Chain(dve, v0, V0, c)
                    k.step(nc.vector.tensor_tensor(res0, xs_hi[:, 0, ds(c * CH, CH)].bitcast(f32),
                                                   xs_lo[:, 0, ds(c * CH, CH)].bitcast(f32), ALU.add))
                    k.wait()
                    k.step(nc.vector.tensor_tensor(t4(res0), t4(res0), row4(bm_row), ALU.add))
                k = chains.get(0)
                if g == 10:
                    wait_ge(dve, merged, c + 1)
                    k.wait()
                    k.step(nc.vector.tensor_tensor(y0, sm[:, 2, :], res0, ALU.add))
                if g == 11:
                    layer_norm_stats(k, y0, D, var0)
                if g == 12:
                    wait_ge(dve, std0, c + 1)
                    normalise(k, y0, y0, D).then_inc(h_nat, 1)
                    assert k.n == V0, k.n
                if g == 14:
                    wait_ge(dve, h_hi_done, c + 1)
                    nc.vector.tensor_tensor(h_lo[:, ds(c * CH, CH)], y0, h_hi[:, ds(c * CH, CH)].bitcast(f32),
                                            ALU.subtract).then_inc(h_lo_done, 1)

            def finish1(g, c):
                nodes = ds(c * TPC, TPC)
                if g == 0:
                    k = chains[0] = Chain(dve, v1, V1, c)
                    wait_ge(dve, masked, (c + 1) * G)
                    nc.vector.tensor_copy(wk_sum, w_acc[:, ds((c % 2) * CH, CH)]).then_inc(wsum_in, 1)
                    nc.vector.tensor_tensor(h_n, h_hi[:, ds(c * CH, CH)].bitcast(f32),
                                            h_lo[:, ds(c * CH, CH)].bitcast(f32), ALU.add).then_inc(hn_sb, 1)
                k = chains.get(0)
                if g == 3:
                    wsum, rec, has, q = (nd[:, i, :] for i in range(4))
                    wait_ge(dve, wsum_ps, c + 1)
                    k.step(nc.vector.tensor_tensor(wsum, sm[:, 3, 0:TPC], ws_fast[:, nodes], ALU.add))
                    k.wait()
                    k.step(nc.vector.tensor_scalar(rec, wsum, EPS, None, ALU.add))
                    k.wait()
                    nc.vector.tensor_scalar(has, wsum, 0.0, None, ALU.is_gt)
                    k.step(nc.vector.reciprocal(rec, rec))
                    k.wait()
                    nc.vector.tensor_tensor(q, rec, r_use[:, nodes], ALU.mult)
                    nc.vector.tensor_tensor(wsum, wsum, rec, ALU.mult)
                    k.step(nc.vector.tensor_scalar(ne[:, nodes], has, -1.0, 1.0, ALU.mult, ALU.add))
                    k.wait()
                    nc.vector.tensor_tensor(qe[:, nodes], q, has, ALU.mult)
                    k.step(nc.vector.tensor_tensor(beta[:, nodes], wsum, ne[:, nodes], ALU.add))
                if g == 4:
                    wait_ge(dve, u_ps, c + 1)
                    k.wait()
                    for t in range(TPC):
                        last = nc.vector.tensor_scalar(u_n[:, t * D:(t + 1) * D], h_n[:, t * D:(t + 1) * D],
                                                       ne[:, ds(c * TPC + t, 1)], None, ALU.mult)
                    k.step(last)
                    k.wait()
                    for t in range(TPC):
                        last = nc.vector.scalar_tensor_tensor(
                            u_n[:, t * D:(t + 1) * D], sm[:, 0, t * D:(t + 1) * D], qe[:, ds(c * TPC + t, 1)],
                            u_n[:, t * D:(t + 1) * D], ALU.mult, ALU.add)
                    last.then_inc(u_sb, 1)
                if g in (7, 8):
                    half = g - 7
                    wait_ge(dve, o1_ps, c * 2 + half + 1)
                    for t in range(2 * half, 2 * half + 2):
                        last = nc.vector.scalar_tensor_tensor(y1[:, t, :], bc1_row[:, :], beta[:, ds(c * TPC + t, 1)],
                                                              pair[:, t, :], ALU.mult, ALU.add)
                    k.step(last)
                    k.wait()
                    for t in range(2 * half, 2 * half + 2):
                        last = nc.vector.tensor_tensor(y1[:, t, :], y1[:, t, :], b_out1, ALU.add)
                    k.step(last)
                if g == 9:
                    layer_norm_stats(k, y1.rearrange("p t n -> p (t n)"), DH, var1)
                if g == 10:
                    wait_ge(dve, std1, c + 1)
                    flat = y1.rearrange("p t n -> p (t n)")
                    normalise(k, flat, flat, DH).then_inc(z_sb, 1)
                if g == 15:
                    wait_ge(dve, g2_sb, c + 1)
                    g2 = sm[:, 2:4, :].rearrange("p a (b m n) -> p (a b) m n", b=2, m=2)
                    for m, (up, low) in enumerate(((t_hi, t_lo), (own_hi, own_lo))):
                        last = nc.vector.tensor_tensor(t4(low[:, ds(c * CH, CH)]), g2[:, :, m, :],
                                                       t4(up[:, ds(c * CH, CH)].bitcast(f32)), ALU.subtract)
                    last.then_inc(t_lo_done, 1)
                    assert k.n == V1, k.n

            def finish2(g, c):
                if g == 0:
                    k = chains[0] = Chain(dve, v2, V2, c)
                    nc.vector.tensor_tensor(h_n, h_hi[:, ds(c * CH, CH)].bitcast(f32),
                                            h_lo[:, ds(c * CH, CH)].bitcast(f32), ALU.add)
                    k.step(nc.vector.tensor_tensor(u_n, own_hi[:, ds(c * CH, CH)].bitcast(f32),
                                                   own_lo[:, ds(c * CH, CH)].bitcast(f32), ALU.add))
                    k.wait()
                    k.step(nc.vector.tensor_tensor(t4(u_n), t4(u_n), row4(b_out2), ALU.add))
                k = chains.get(0)
                if g == 1:
                    k.wait()
                    for t in range(TPC):
                        last = nc.vector.scalar_tensor_tensor(
                            u_n[:, t * D:(t + 1) * D], bc2_row, beta[:, ds(c * TPC + t, 1)],
                            u_n[:, t * D:(t + 1) * D], ALU.mult, ALU.add)
                    k.step(last)
                if g in (2, 3):
                    k.wait()
                    for t in range(TPC):
                        last = nc.vector.scalar_tensor_tensor(
                            u_n[:, t * D:(t + 1) * D],
                            (t_hi, t_lo)[g - 2][:, ds(c * CH + t * D, D)].bitcast(f32),
                            ne[:, ds(c * TPC + t, 1)], u_n[:, t * D:(t + 1) * D], ALU.mult, ALU.add)
                    k.step(last)
                if g == 5:
                    wait_ge(dve, t_ps, c + 1)
                    k.wait()
                    for t in range(TPC):
                        last = nc.vector.scalar_tensor_tensor(
                            u_n[:, t * D:(t + 1) * D], sm[:, 0, t * D:(t + 1) * D], qe[:, ds(c * TPC + t, 1)],
                            u_n[:, t * D:(t + 1) * D], ALU.mult, ALU.add)
                    k.step(last)
                if g == 6:
                    layer_norm_stats(k, u_n, D, var2)
                if g == 7:
                    wait_ge(dve, std2, c * 2 + 1)
                    k.step(normalise(k, z2, u_n, D))
                if g == 8:
                    k.wait()
                    k.step(nc.vector.tensor_tensor(t4(z2), t4(z2), row4(g2_row), ALU.mult))
                    k.wait()
                    k.step(nc.vector.tensor_tensor(t4(z2), t4(z2), row4(be2_row), ALU.add))
                if g == 9:
                    k.wait()
                    k.step(nc.vector.scalar_tensor_tensor(z2, z2, 0.0, h_n, ALU.max, ALU.add))
                    layer_norm_stats(k, z2, D, var2)
                if g == 10:
                    wait_ge(dve, std2, c * 2 + 2)
                    wait_ge(dve, out_done, c * 16 + 16)
                    normalise(k, z3, z2, D).then_inc(out_sb, 1)
                    assert k.n == V2, k.n

            def chunk0(c):
                for g in range(G):
                    split(0, c, g)
                    if not isinstance(c, int):
                        finish0(g, c - 1)
            sweep(dve, chunk0)

            dve.wait_ge(hi_done, XT + TILES)
            dve.wait_ge(count_done, TILES)
            nc.vector.tensor_reduce(s_all[:, :], s_part[:, :].rearrange("p (k c) -> p k c", c=NCH),
                                    axis=AX.X, op=ALU.add).then_inc(totals, 1)
            dve.wait_ge(totals, 1)
            nc.vector.tensor_scalar(over[:, :], s_all[:, :], SUM_LIMIT, None, ALU.is_ge)
            nc.vector.tensor_scalar(r_all[:, :], s_all[:, :], EPS, None, ALU.add).then_inc(totals, 1)
            dve.wait_ge(totals, 2)
            nc.vector.reciprocal(r_all[:, :], r_all[:, :])
            nc.vector.tensor_reduce(small_n[:, TILES:TILES + 1], over[:, :], axis=AX.X, op=ALU.add)\
                .then_inc(totals, 1)
            dve.wait_ge(totals, 3)
            nc.vector.tensor_reduce(bad[:, 0:1], small_n[:, :], axis=AX.X, op=ALU.add).then_inc(totals, 1)
            dve.wait_ge(flag_ps, 1)
            nc.vector.tensor_scalar(flag_i[:, :], sm[:, 3, 0:1], 0.0, None, ALU.is_gt)
            nc.vector.tensor_scalar(bad[:, 1:2], sm[:, 3, 0:1], 0.0, None, ALU.is_gt)
            nc.vector.tensor_scalar(bad[:, 2:3], sm[:, 3, 0:1], 0.0, None, ALU.is_le)
            nc.vector.tensor_copy(r_rows[:, :], sm[0:TN, 3, 128:256]).then_inc(r_rows_sb, 1)
            dve.wait_ge(r_rows_sb, 1)
            nc.vector.tensor_scalar(r_use[:, :], r_all[:, :], bad[:, 2:3], bad[:, 1:2], ALU.mult, ALU.add)
            nc.vector.scalar_tensor_tensor(ws_fast[:, :], s_all[:, :], bad[:, 2:3], r_all[:, :],
                                           ALU.mult, ALU.mult).then_inc(flag_v, 1)
            dve.wait_ge(flag_v, 1)
            flag = dve.value_load(flag_i[0:1, 0:1], min_val=0, max_val=1)

            for g in range(LOOK):
                mask(1, 0, g, flag)
            for p in (1, 2):
                def chunk(c, p=p, last=False):
                    first = isinstance(c, int) and c == 0
                    for g in range(G):
                        if g + LOOK < G:
                            mask(p, c, g + LOOK, flag)
                        elif not last:
                            mask(p, c + 1, g + LOOK - G, flag)
                        elif p == 1:
                            mask(2, 0, g + LOOK - G, flag)
                        split(p, c, g)
                        if first:
                            (finish0 if p == 1 else finish1)(g, NCH - 1)
                        else:
                            (finish1 if p == 1 else finish2)(g, c - 1)
                chunk(0)
                with dve.Fori(1, NCH - 1) as c:
                    chunk(c)
                chunk(NCH - 1, last=True)
            for g in range(G):
                finish2(g, NCH - 1)

        @block.tensor
        def _(pe):
            pe.wait_ge(w_in, 16 * 12)
            pe.wait_ge(setup, 1)
            w_in1t = axA[:, 0:DH].rearrange("p (a n) -> p a n", a=2)
            w_out1 = m1A.rearrange("p (a n) -> p a n", a=2)
            w_out2 = y0[:, 0:D]
            for a in range(2):
                nc.tensor.matmul(sm[:, 0, 0:DH], w_in1t[:, a, :], w_out1[:, a, :], start=a == 0, stop=a == 1)
            for a in range(2):
                nc.tensor.matmul(sm[:, 1, 0:DH], col_rep[:, a, :], w_out1[:, a, :], start=a == 0, stop=a == 1)
            for a in range(2):
                nc.tensor.matmul(sm[:, 2, a * D:(a + 1) * D], w_in2t[:, a, :], w_out2, start=True, stop=True)
            nc.tensor.matmul(sm[:, 3, 0:D], col_rep[:, 2, :], w_out2, start=True, stop=True).then_inc(prod_ps, 1)

            def aggregate(p, c, g):
                feats = [(xs_hi[:, 0, :], xs_lo[:, 0, :]), (xs_hi[:, 1, :], xs_lo[:, 1, :])] if p == 0 \
                    else [(h_hi[:, :], h_lo[:, :])] if p == 1 else [(t_hi, t_lo)]
                if p == 0 and isinstance(c, int) and g % 4 == 0:
                    pe.wait_ge(lo_done, 2 * (g // 4) + 2)
                ts = [g * KT + k for k in range(KT)]
                if p and isinstance(c, int) and ts[0] in (0, TPC * (NCH - 1)):
                    pe.wait_ge(h_lo_done if p == 1 else t_lo_done, NCH if g else NCH - 1)
                slot = g % NSPLIT
                wait_ge(pe, hi_done, at(p, c, g) + 1)
                last = None

                def product(f, weights, moving, t, k, first, final):
                    bank = (c % 2) * CH + f * 2 * CH
                    return nc.tensor.matmul(big[:, ds(bank, CH)], weights[:, t * D:(t + 1) * D],
                                            moving[:, slot, k * CH:(k + 1) * CH], start=first, stop=final)
                for k, t in enumerate(ts):
                    for f, (w_hi, w_lo) in enumerate(feats):
                        product(f, w_hi, hi, t, k, g == 0 and k == 0, False)
                        product(f, w_lo, hi, t, k, False, False)
                wait_ge(pe, lo_done, at(p, c, g) + 1)
                for k, t in enumerate(ts):
                    for f, (w_hi, w_lo) in enumerate(feats):
                        last = product(f, w_hi, lo, t, k, False, g == G - 1 and k == KT - 1)
                last.then_inc(used, 1)

            def finish0(g, c):
                if g in (1, 3, 5):
                    layer = (g - 1) // 2
                    if layer == 0:
                        wait_ge(pe, agg_out, c + 1)
                    else:
                        wait_ge(pe, mlp_sb, c * LAYERS + layer)
                    src = ((axA, axB), (m1A, m1B))[layer % 2]
                    for b in range(2):
                        last = nc.tensor.matmul(sm[:, b, :], mlp[:, b * LAYERS + layer, :], src[b],
                                                start=True, stop=True)
                    last.then_inc(mlp_ps, 1)
                if g == 7:
                    wait_ge(pe, mlp_sb, c * LAYERS + LAYERS)
                    for t in range(TPC):
                        for b, src in enumerate((m1A, m1B)):
                            last = nc.tensor.matmul(sm[:, 2, t * D:(t + 1) * D], src[:, t * D:(t + 1) * D],
                                                    merge[:, b, :], start=b == 0, stop=b == 1)
                    last.then_inc(merged, 1)

            def finish1(g, c):
                if g == 0:
                    wait_ge(pe, wsum_in, c + 1)
                    for t in range(TPC):
                        last = nc.tensor.matmul(sm[:, 3, t:t + 1], wk_sum[:, t * D:(t + 1) * D], ones[:, 0:1],
                                                start=True, stop=True)
                    last.then_inc(wsum_ps, 1)
                    wait_ge(pe, agg_out, c + NCH + 1)
                    for t in range(TPC):
                        last = nc.tensor.transpose(sm[:, 0, t * D:(t + 1) * D], ut[:, t * D:(t + 1) * D], ident[:, :])
                    last.then_inc(u_ps, 1)
                if g == 2:
                    wait_ge(pe, u_sb, c + 1)
                    for t in range(TPC):
                        nc.tensor.transpose(sm[:, 1, t * D:(t + 1) * D], u_n[:, t * D:(t + 1) * D], ident[:, :])
                    for t in range(TPC):
                        last = nc.tensor.transpose(sm[:, 2, t * D:(t + 1) * D], h_n[:, t * D:(t + 1) * D], ident[:, :])
                    last.then_inc(ut_ps, 1)
                if g in (4, 5):
                    half = g - 4
                    wait_ge(pe, ut_sb, c + 1)
                    for t in range(2 * half, 2 * half + 2):
                        nc.tensor.matmul(pair[:, t, :], u_t[:, t * D:(t + 1) * D], w_c1[:, :], start=True, stop=False)
                        last = nc.tensor.matmul(pair[:, t, :], h_t[:, t * D:(t + 1) * D], w_self1[:, :],
                                                start=False, stop=True)
                    last.then_inc(o1_ps, 1)
                if g == 9:
                    wait_ge(pe, z_sb, c + 1)
                    for b in range(2):
                        for t in range(TPC):
                            last = nc.tensor.transpose(sm[:, b, t * D:(t + 1) * D], y1[:, t, b * D:(b + 1) * D],
                                                       ident[:, :])
                    last.then_inc(z_ps, 1)
                if g in (10, 11):
                    half = g - 10
                    wait_ge(pe, h2_sb, c + 1)
                    for t in range(2 * half, 2 * half + 2):
                        for b in range(2):
                            last = nc.tensor.matmul(sm[:, 2 + half, (t % 2) * DH:(t % 2 + 1) * DH],
                                                    h2t[:, b, t * D:(t + 1) * D],
                                                    w_2[:, b, :, :].rearrange("p a n -> p (a n)"),
                                                    start=b == 0, stop=b == 1)
                    if half:
                        last.then_inc(g2_ps, 1)

            def finish2(g, c):
                if g == 1:
                    wait_ge(pe, agg_out, c + 2 * NCH + 1)
                    for t in range(TPC):
                        last = nc.tensor.transpose(sm[:, 0, t * D:(t + 1) * D], ut[:, t * D:(t + 1) * D], ident[:, :])
                    last.then_inc(t_ps, 1)

            finish = (finish0, finish1, finish2)
            pe.wait_ge(prod_sb, 1)
            for p in range(3):
                def chunk(c, p=p):
                    first = isinstance(c, int)
                    for g in range(G):
                        aggregate(p, c, g)
                        if first and p:
                            finish[p - 1](g, NCH - 1)
                        elif not first:
                            finish[p](g, c - 1)
                sweep(pe, chunk)
                if p == 0:
                    pe.wait_ge(totals, 4)
                    nc.tensor.matmul(sm[:, 3, 0:1], ones[:, :], bad[:, 0:1], start=True, stop=True)
                    nc.tensor.transpose(sm[0:TN, 3, 128:256], r_all[:, :], ident[:, :]).then_inc(flag_ps, 1)
            for g in range(G):
                finish2(g, NCH - 1)


def kernel(**inputs):
    import concourse.bacc as _bacc
    from concourse.bass_utils import run_bass_kernel_spmd as _run

    a = {k: np.asarray(v) for k, v in inputs.items()}
    adj = a["adj"]

    def blocks(m):
        return np.ascontiguousarray(
            m.reshape(G, KT, 128, NCH, CH).transpose(3, 0, 2, 1, 4)).reshape(NCH * G, 128, LOAD)

    def nodes(x):
        return np.ascontiguousarray(x.reshape(TN, 128, D).transpose(1, 0, 2)).reshape(128, N)

    def halves(w):
        return np.ascontiguousarray(w.reshape(2, 128, -1).transpose(1, 0, 2))

    p0, p1 = "L0_gnn_", "L1_gnn_"
    mlp_w = np.stack([w for b in ("W1", "W2") for w in a[p0 + b]]).transpose(2, 0, 1)
    merge_w = halves(a[p0 + "Wm"].T)
    cols = np.concatenate([
        a[p0 + "b1"].T, a[p0 + "b2"].T, a[p1 + "g1"].reshape(2, 128).T, a[p1 + "be1"].reshape(2, 128).T,
        a[p1 + "b_in1"].reshape(2, 128).T, a[p1 + "b_in2"].reshape(128, 1)], axis=1)
    rows = np.concatenate([a[p0 + "bm"], a[p1 + "g2"], a[p1 + "be2"], a[p1 + "b_out2"], a[p1 + "b_self2"],
                           np.zeros(2 * D, np.float32), a[p1 + "b_out1"], a[p1 + "b_self1"]])
    arrays = {
        "adj_rows": blocks(adj.T), "adj_cols": blocks(adj), "x_in": nodes(a["x"]), "x2_in": nodes(a[p0 + "x2"]),
        "mlp_w": mlp_w, "merge_w": merge_w, "win1_t": halves(a[p1 + "W_in1"].T).reshape(128, DH),
        "wout1": halves(a[p1 + "W_out1"]).reshape(128, 512), "wself1": a[p1 + "W_self1"],
        "win2_t": a[p1 + "W_in2"].T.reshape(128, 2, 128), "wout2": a[p1 + "W_out2"], "wself2": halves(a[p1 + "W_self2"]),
        "cols_in": cols, "rows_in": rows, "eps_in": np.concatenate([a[p0 + "eps1"], a[p0 + "eps2"]]),
        "ident_in": np.eye(128, dtype=np.float32),
    }
    arrays = {k: np.ascontiguousarray(v) for k, v in arrays.items()}
    nc = _bacc.Bacc("TRN2", target_bir_lowering=False, num_devices=1, dynamic_dma_scratch_size=8192)
    f32 = mybir.dt.float32
    args = {k: nc.dram_tensor(k, v.shape, f32, kind="ExternalInput").ap() for k, v in arrays.items()}
    args["r_dram"] = nc.dram_tensor("r_dram", (TN, 128), f32).ap()
    args["out"] = nc.dram_tensor("out", (NCH, 128, CH), f32, kind="ExternalOutput").ap()
    gnn_kernel(nc, **args)
    r = _run(nc, [arrays], core_ids=[0])
    got = np.asarray(r.results[0]["out"])
    return np.ascontiguousarray(got.reshape(NCH, 128, TPC, 128).transpose(0, 2, 1, 3)).reshape(N, D)
```

```python
import numpy as np
import concourse.bass as bass
from concourse import mybir
from contextlib import ExitStack

N = 4096
D = 128
DH = 256
LAYERS = 3
TN = N // D
CH = 512
NCH = N // CH
TPC = CH // D
KT = 2
G = TN // KT
XT = 2 * TN // 8
TILES = NCH * G
LOAD = KT * CH
NRAW = 8
NSPLIT = 4
LOOK = 2
THRESH = 1e-06
EPS = 1e-08
LN_EPS = 1e-05
SMALL = 2 * THRESH * N
SUM_LIMIT = 1.5 * N


def gnn_kernel(nc, adj_rows, adj_cols, x_in, x2_in, mlp_w, merge_w, win1_t, wout1, wself1,
               win2_t, wout2, wself2, cols_in, rows_in, eps_in, ident_in, r_dram, out):
    f32, f32r, i32 = mybir.dt.float32, mybir.dt.float32r, mybir.dt.int32
    ALU, ACT, AX = mybir.AluOpType, mybir.ActivationFunctionType, mybir.AxisListType
    ds = bass.ds
    ctx = ExitStack()
    with ctx:
        def sb(name, shape, dt=f32):
            return ctx.enter_context(nc.sbuf_tensor(name, shape, dt))

        def sem(name):
            return ctx.enter_context(nc.semaphore(name))

        raw = sb("raw", [128, NRAW, LOAD])
        hi = sb("hi", [128, NSPLIT, LOAD], f32r)
        lo = sb("lo", [128, NSPLIT, LOAD], f32r)
        xs_hi = sb("xs_hi", [128, 2, N], f32r)
        xs_lo = sb("xs_lo", [128, 2, N], f32r)
        h_hi = sb("h_hi", [128, N], f32r)
        h_lo = sb("h_lo", [128, N], f32r)
        t_hi, t_lo = xs_hi[:, 0, :], xs_lo[:, 0, :]
        own_hi, own_lo = xs_hi[:, 1, :], xs_lo[:, 1, :]

        mlp = sb("mlp", [128, 2 * LAYERS, D])
        merge = sb("merge", [128, 2, D])
        w_self1 = sb("w_self1", [128, DH])
        w_c1 = sb("w_c1", [128, DH])
        w_2 = sb("w_2", [128, 2, 2, D])
        w_in2t = sb("w_in2t", [128, 2, D])
        bias_cols = sb("bias_cols", [128, 13])
        bias_rows = sb("bias_rows", [128, 7 * D + 2 * DH])
        bm_row = bias_rows[:, 0:D]
        g2_row = bias_rows[:, D:2 * D]
        be2_row = bias_rows[:, 2 * D:3 * D]
        b_out2 = bias_rows[:, 3 * D:4 * D]
        b_self2 = bias_rows[:, 4 * D:5 * D]
        out2_rows = bias_rows[:, 5 * D:7 * D]
        b_out1 = bias_rows[:, 7 * D:7 * D + DH]
        b_self1 = bias_rows[:, 7 * D + DH:7 * D + 2 * DH]
        bc1_row = sb("bc1_row", [128, DH])
        col_rep = sb("col_rep", [128, 3, 128])
        scale = sb("scale", [128, 2])
        ident = sb("ident", [128, 128])
        ident_r = sb("ident_r", [128, 128], f32r)
        rows01 = sb("rows01", [128, 128], f32r)
        add1 = sb("add1", [128, DH], f32r)
        add2 = sb("add2", [128, DH], f32r)
        part0 = sb("part0", [128, 2])
        ones = sb("ones", [128, 128])

        wk = sb("wk", [128, 8, CH])
        axA, axB, m1A, m1B = wk[:, 0, :], wk[:, 1, :], wk[:, 2, :], wk[:, 3, :]
        res0, y0 = wk[:, 4, :], wk[:, 5, :]
        ut, u_n, h_t = wk[:, 0, :], wk[:, 1, :], wk[:, 3, :]
        h_n = wk[:, 4, :]
        y1 = wk[:, 5:7, :].rearrange("p a (b n) -> p (a b) n", b=2)
        wk_sum = wk[:, 7, :]
        h2t = sb("h2t", [128, 2, CH])
        z2 = h2t[:, 0, :]
        z3 = h2t[:, 1, :]
        stats = sb("stats", [128, TPC, 6])
        mv = sb("mv", [128, TPC, 2])
        ln_eps = sb("ln_eps", [128, TPC])
        half_power = sb("half_power", [128, TPC])
        rstd = sb("rstd", [128, TPC])
        shift = sb("shift", [128, TPC])
        nd = sb("nd", [128, 4, TN])
        s_part = sb("s_part", [128, TN * NCH])
        small_n = sb("small_n", [128, TILES + 1])
        s_all = sb("s_all", [128, TN])
        r_all = sb("r_all", [128, TN])
        ws_fast = sb("ws_fast", [128, TN])
        over = sb("over", [128, 2 * TN])
        bad = sb("bad", [128, 1])
        flag_i = sb("flag_i", [128, 1], i32)
        qe = sb("qe", [128, TN])
        ne = sb("ne", [128, TN])
        beta = sb("beta", [128, TN])
        r_rows = sb("r_rows", [TN, 128])
        rb = sb("rb", [128, 2 * CH])
        w_acc = sb("w_acc", [128, 2 * CH])

        big = ctx.enter_context(nc.psum_tensor("big", [128, 4 * CH], f32))
        sm = ctx.enter_context(nc.psum_tensor("sm", [128, 4, CH], f32))
        pair = big[:, 2 * CH:4 * CH].rearrange("p (t n) -> p t n", n=DH)

        raw_in = [sem(f"raw_in{s}") for s in range(NRAW)]
        w_in = sem("w_in")
        setup = sem("setup")
        prod_ps = sem("prod_ps")
        biases = sem("biases")
        prod_sb = sem("prod_sb")
        masked = sem("masked")
        gen = sem("gen")
        hi_done = sem("hi_done")
        count_done = sem("count_done")
        lo_done = sem("lo_done")
        x_lo_done = sem("x_lo_done")
        used = sem("used")
        agg_out = sem("agg_out")
        mlp_ps = sem("mlp_ps")
        mlp_sb = sem("mlp_sb")
        merged = sem("merged")
        v0 = sem("v0")
        v1 = sem("v1")
        v2 = sem("v2")
        var0 = sem("var0")
        inv0 = sem("inv0")
        h_nat = sem("h_nat")
        h_hi_done = sem("h_hi_done")
        h_lo_done = sem("h_lo_done")
        totals = sem("totals")
        flag_ps = sem("flag_ps")
        flag_v = sem("flag_v")
        r_rows_sb = sem("r_rows_sb")
        r_stored = sem("r_stored")
        rb_in = sem("rb_in")
        wsum_in = sem("wsum_in")
        wsum_ps = sem("wsum_ps")
        node_v = sem("node_v")
        u_ps = sem("u_ps")
        ht_ps = sem("ht_ps")
        ht_sb = sem("ht_sb")
        self_ps = sem("self_ps")
        self_sb = sem("self_sb")
        lone_ps = sem("lone_ps")
        lone_steps = sem("lone_steps")
        u_scaled = sem("u_scaled")
        u_sb = sem("u_sb")
        ut_ps = sem("ut_ps")
        ut_sb = sem("ut_sb")
        hn_sb = sem("hn_sb")
        o1_ps = sem("o1_ps")
        var1 = sem("var1")
        inv1 = sem("inv1")
        rstd2 = sem("rstd2")
        z2_sb = sem("z2_sb")
        y2_ps = sem("y2_ps")
        z_sb = sem("z_sb")
        z_ps = sem("z_ps")
        h2_sb = sem("h2_sb")
        g2_ps = sem("g2_ps")
        g2_sb = sem("g2_sb")
        t_lo_done = sem("t_lo_done")
        t_ps = sem("t_ps")
        node_steps = sem("node_steps")
        own_steps = sem("own_steps")
        var2 = sem("var2")
        inv2 = sem("inv2")
        out_sb = sem("out_sb")
        passed = sem("passed")
        out_done = sem("out_done")
        pool_steps = sem("pool_steps")

        class Chain:

            def __init__(self, eng, s, per_chunk, c):
                self.eng, self.sem, self.k, self.c, self.n = eng, s, per_chunk, c, 0

            def step(self, ins):
                self.n += 1
                ins.then_inc(self.sem, 1)

            def wait(self):
                wait_ge(self.eng, self.sem, self.c * self.k + self.n)

        def wait_ge(eng, s, value):
            assert not isinstance(value, int) or value > 0
            eng.wait_ge(s, value)

        A0_AX, P0_MLP, A0_MLP, P0_MERGE = 2, (1, 3, 5), (5, 7, 9), 7
        V0_RES, V0_Y, V0_ST, V0_NORM, A0_H, V0_H = 6, 10, 11, 11, 12, 12
        A_HT, A_SELF, A_UT, P_HT, P_SELF, P_OUT = 2, (6, 8), 0, 0, (1, 3), (0, 5)
        V_Y1, V_ST, V_NORM = (6, 8), (6, 8), (8, 10)
        P_LONE = 6
        assert P_LONE <= V_Y1[0] and A_SELF[1] <= V_Y1[0] + LOOK and A_SELF[1] < P_LONE + NSPLIT
        P_Z, A_H2, P_G2, A_G2, V_G2 = (8, 10), (11, 14), (10, 12), (14, 15), 15
        A2_UT, P2_T, P2_Y, A2_SCALE, V2_Y, V2_ST, V2_SHIFT, A2_NORM = 3, 1, 3, 6, 6, 6, 8, 10
        V2_AGGR, V2_AGGR2, V_AGGR, S_WEIGHTS, V_SETUP, P_PRODUCTS, A_PRODUCTS, V_BIASES = 6, 12, (7, 9), 10, 9, 10, 15, 14
        V2_GAMMA, V2_BETA, V2_RELU, V2_ST2, V2_OUT, A2_FINAL, A2_OUT = 10, 10, 11, 12, 13, 15, 15
        V0, V1, V2 = 4, 4, 6

        def tile(p, c, g):
            return c * G + (p * TILES + g)

        def at(p, c, g):
            if p == 0 and isinstance(c, int) and c == 0:
                return tile(p, c, g) + 2 * (g // 4 + 1)
            return tile(p, c, g) + XT

        def aggregated(eng, p, c):
            wait_ge(eng, used, c * G + (p * TILES + G))

        def slot_of(p, c, g):
            return (at(p, c, g) if p == 0 and isinstance(c, int) else g) % NRAW

        def uses(p, c, g):
            return at(p, c, g) // NRAW + 1 if isinstance(c, int) \
                else c * (G // NRAW) + ((XT + p * TILES + g) // NRAW + 1)

        FEATURES = [(part, b, 6 * part + b) for part in range(XT // 2) for b in range(2)]
        FIRST_X = 2

        def low_features(eng, ops, which):
            for i in which:
                part, b, n = FEATURES[i]
                cols = slice(part * LOAD, (part + 1) * LOAD)
                eng.wait_ge(hi_done, n + 1)
                ops.tensor_tensor(xs_lo[:, b, cols], raw[:, n % NRAW, :], xs_hi[:, b, cols].bitcast(f32),
                                  ALU.subtract).then_inc(x_lo_done, 1)

        block = ctx.enter_context(nc.Block())

        def sweep(eng, body):
            body(0)
            with eng.Fori(1, NCH) as c:
                body(c)

        @block.sync
        def _(sp):
            def load_weights():
                for dst, src in ((mlp[:, :, :], mlp_w), (merge[:, :, :], merge_w), (w_self1[:, :], wself1),
                                 (w_2[:, :, 1, :], wself2), (w_in2t[:, :, :], win2_t), (ident[:, :], ident_in),
                                 (bias_cols[:, :], cols_in),
                                 (bias_rows[:, :], rows_in.partition_broadcast(128)),
                                 (scale[:, :], eps_in.partition_broadcast(128)),
                                 (axA[:, 0:DH], win1_t), (m1A, wout1), (y0[:, 0:D], wout2)):
                    sp.dma_start(dst, src).then_inc(w_in, 16)

            def slot_is_free(n):
                part, place = n // 6, n % 6
                if place < 2:
                    sp.wait_ge(x_lo_done, 2 * part + place + 1)
                else:
                    sp.wait_ge(lo_done, 4 * part + place - 1)

            def load_features(g):
                for part, b, n in FEATURES:
                    if 4 * part == g:
                        if n >= NRAW:
                            slot_is_free(n - NRAW)
                        sp.dma_start(raw[:, n % NRAW, :], (x_in, x2_in)[b][:, part * LOAD:(part + 1) * LOAD])\
                          .then_inc(raw_in[n % NRAW], 16)

            for p in range(3):
                def loads(c, p=p):
                    for g in range(G):
                        first = p == 0 and isinstance(c, int)
                        if first:
                            load_features(g)
                            if g == S_WEIGHTS:
                                load_weights()
                        if not first or c:
                            if g == 2:
                                sp.wait_ge(x_lo_done, XT)
                            wait_ge(sp, lo_done, tile(p, c, g) - NRAW + (3 if g < 2 else 1))
                        elif at(p, c, g) >= NRAW:
                            slot_is_free(at(p, c, g) - NRAW)
                        src = (adj_rows if p == 0 else adj_cols)[ds(c * G + g, 1)]
                        s = slot_of(p, c, g)
                        sp.dma_start(raw[:, s, :], src.rearrange("a p n -> p (a n)")).then_inc(raw_in[s], 16)
                sweep(sp, loads)

            sp.wait_ge(out_done, 16 * NCH + 16)

        @block.gpsimd
        def _(pool):
            pool.wait_ge(x_lo_done, FIRST_X)
            low_features(pool, nc.gpsimd, range(FIRST_X, XT))
            def inverse_deviation(var, inv, n, earlier, tiles=slice(0, TPC)):
                wait_ge(pool, var, n)
                nc.gpsimd.tensor_tensor(rstd[:, tiles], mv[:, tiles, 1], ln_eps[:, tiles], ALU.add).then_inc(pool_steps, 1)
                wait_ge(pool, pool_steps, n + (1 + earlier))
                nc.gpsimd.tensor_tensor(rstd[:, tiles], rstd[:, tiles], half_power[:, tiles], ALU.pow)\
                    .then_inc(inv, 1)

            halves = slice(0, TPC // 2), slice(TPC // 2, TPC)

            def load_row(n):
                if not isinstance(n, int) or n > 0:
                    wait_ge(pool, rb_in, n * 16)
                if not isinstance(n, int) or n > 1:
                    wait_ge(pool, lo_done, n * G + tile(1, -1, 0))
                src = r_dram[ds((n % NCH) * TPC, TPC), :].rearrange("t n -> (t n)")
                pool.dma_start(rb[:, ds((n % 2) * CH, CH)], src.partition_broadcast(128)).then_inc(rb_in, 16)

            nc.gpsimd.memset(ln_eps[:, :], LN_EPS)
            nc.gpsimd.memset(half_power[:, :], -0.5).then_inc(pool_steps, 1)
            pool.wait_ge(pool_steps, 1)
            inverse_deviation(var0, inv0, 1, 0)
            with pool.Fori(1, NCH - 1) as c:
                inverse_deviation(var0, inv0, c + 1, 0)
            pool.wait_ge(r_rows_sb, 1)
            pool.dma_start(r_dram, r_rows[:, :]).then_inc(r_stored, 16)
            pool.wait_ge(r_stored, 16)
            load_row(0)
            load_row(1)
            inverse_deviation(var0, inv0, NCH, 0)
            with pool.Fori(2, NCH + 2) as n:
                load_row(n)
                for half in range(2):
                    inverse_deviation(var1, inv1, n * 2 + (half - 3), NCH, halves[half])
            with pool.Fori(NCH + 2, 2 * NCH) as n:
                load_row(n)
                for k in range(2):
                    inverse_deviation(var2, inv2, n * 2 + (k - 2 * NCH - 3), 3 * NCH)
            for n in range(2 * (NCH - 2), 2 * NCH):
                inverse_deviation(var2, inv2, n + 1, 3 * NCH)
            pool.wait_ge(rb_in, 16 * 2 * NCH)

        @block.scalar
        def _(act):
            def split_features(g):
                for part, b, n in FEATURES:
                    if 4 * part == g:
                        act.wait_ge(raw_in[n % NRAW], 16 * (n // NRAW + 1))
                        nc.scalar.activation(xs_hi[:, b, part * LOAD:(part + 1) * LOAD], raw[:, n % NRAW, :],
                                             ACT.Copy).then_inc(hi_done, 1)

            def copy_products():
                act.wait_ge(setup, 1)
                act.wait_ge(prod_ps, 1)
                nc.scalar.copy(w_c1[:, :], sm[:, 0, 0:DH])
                nc.scalar.copy(bc1_row[:, :], sm[:, 1, 0:DH])
                nc.scalar.copy(w_2[:, :, 0, :], sm[:, 2, 0:2 * D].rearrange("p (a n) -> p a n", a=2))
                nc.scalar.copy(out2_rows[:, 0:D], sm[:, 3, 0:D]).then_inc(prod_sb, 1)

            def split(p, c, g):
                if p == 0 and isinstance(c, int):
                    split_features(g)
                wait_ge(act, raw_in[slot_of(p, c, g)], 16 * uses(p, c, g))
                if p:
                    wait_ge(act, masked, c * G + ((p - 1) * TILES + g + 1))
                if not (p == 0 and isinstance(c, int) and g < NSPLIT):
                    wait_ge(act, used, tile(p, c, g) - NSPLIT + 1)
                dst = hi[:, g % NSPLIT, :]
                src = raw[:, slot_of(p, c, g), :]
                if p:
                    nc.scalar.activation(dst, src, ACT.Copy).then_inc(hi_done, 1)
                    return
                for k in range(KT):
                    last = nc.scalar.activation(dst[:, k * CH:(k + 1) * CH], src[:, k * CH:(k + 1) * CH], ACT.Copy,
                                                accum_out=s_part[:, ds(c + (g * KT + k) * NCH, 1)])
                last.then_inc(hi_done, 1)

            def normalise(dst, y, width):
                for t in range(TPC):
                    cols = slice(t * width, (t + 1) * width)
                    last = nc.scalar.activation(dst[:, cols], y[:, cols], ACT.Identity, scale=rstd[:, t:t + 1],
                                                bias=shift[:, t:t + 1])
                return last

            def scale_nodes(c):
                for t in range(TPC):
                    last = nc.scalar.activation(u_n[:, t * D:(t + 1) * D], sm[:, 0, t * D:(t + 1) * D], ACT.Copy,
                                                scale=qe[:, ds(c * TPC + t, 1)])
                last.then_inc(u_scaled, 1)

            def finish0(g, c):
                if g == A0_AX:
                    aggregated(act, 0, c)
                    bank = (c % 2) * CH
                    nc.scalar.activation(axA, big[:, ds(bank, CH)], ACT.Copy, scale=scale[:, 0:1])
                    nc.scalar.activation(axB, big[:, ds(bank + 2 * CH, CH)], ACT.Copy,
                                         scale=scale[:, 1:2]).then_inc(agg_out, 1)
                if g in A0_MLP:
                    layer = A0_MLP.index(g)
                    wait_ge(act, mlp_ps, c * LAYERS + layer + 1)
                    dst = ((m1A, m1B), (axA, axB))[layer % 2]
                    for b in range(2):
                        last = nc.scalar.activation(dst[b], sm[:, b, :], ACT.Relu,
                                                    bias=bias_cols[:, b * LAYERS + layer:b * LAYERS + layer + 1])
                    last.then_inc(mlp_sb, 1)
                if g == A0_H:
                    wait_ge(act, h_nat, c + 1)
                    nc.scalar.activation(h_hi[:, ds(c * CH, CH)], y0, ACT.Copy).then_inc(h_hi_done, 1)

            def finish1(g, c):
                if g == A_UT:
                    aggregated(act, 1, c)
                    nc.scalar.activation(ut, big[:, ds((c % 2) * CH, CH)], ACT.Copy).then_inc(agg_out, 1)
                if g == A_HT:
                    wait_ge(act, ht_ps, c + 1)
                    nc.scalar.activation(h_t, sm[:, 2, :], ACT.Copy).then_inc(ht_sb, 1)
                if g in A_SELF:
                    half = A_SELF.index(g)
                    wait_ge(act, self_ps, c * 2 + half + 1)
                    nc.scalar.activation(y1[:, 2 * half:2 * half + 2, :], pair[:, 2 * half:2 * half + 2, :], ACT.Copy)\
                        .then_inc(self_sb, 1)
                if g in A_H2:
                    half = A_H2.index(g)
                    wait_ge(act, z_ps, c * 2 + half + 1)
                    cols = slice(half * DH, (half + 1) * DH)
                    for b in range(2):
                        last = nc.scalar.activation(h2t[:, b, cols], sm[:, half, b * DH:(b + 1) * DH], ACT.Relu,
                                                    scale=bias_cols[:, 6 + b:7 + b], bias=bias_cols[:, 8 + b:9 + b])
                    last.then_inc(h2_sb, 1)
                for half in (h for h in range(2) if A_G2[h] == g):
                    wait_ge(act, g2_ps, c * 2 + half + 1)
                    g2 = sm[:, 2 + half, :].rearrange("p (b m n) -> p b m n", b=2, m=2)
                    for m, dst in enumerate((t_hi, own_hi)):
                        last = nc.scalar.activation(dst[:, ds(c * CH + half * DH, DH)].rearrange("p (t n) -> p t n", n=D),
                                                    g2[:, :, m, :], ACT.Copy)
                    last.then_inc(g2_sb, 1)

            def finish2(g, c):
                if g == A2_UT:
                    aggregated(act, 2, c)
                    nc.scalar.activation(ut, big[:, ds((c % 2) * CH, CH)], ACT.Copy).then_inc(agg_out, 1)
                if g == A2_SCALE:
                    wait_ge(act, t_ps, c + 1)
                    scale_nodes(c)
                if g == A2_NORM:
                    wait_ge(act, rstd2, c * 2 + 1)
                    if not isinstance(c, int) or c:
                        wait_ge(act, out_sb, c)
                    normalise(z2, u_n, D).then_inc(z2_sb, 1)
                if g == A2_FINAL:
                    wait_ge(act, rstd2, c * 2 + 2)
                    wait_ge(act, out_done, c * 16 + 16)
                    normalise(z3, z2, D).then_inc(out_sb, 1)
                if g == A2_OUT:
                    wait_ge(act, out_sb, c + 1)
                    act.dma_start(out[ds(c, 1)].rearrange("a p n -> p (a n)"), z3).then_inc(out_done, 16)

            finish = (finish0, finish1, finish2)
            for p in range(3):
                def chunk(c, p=p):
                    first = isinstance(c, int)
                    for g in range(G):
                        split(p, c, g)
                        if first and p == 0 and g == A_PRODUCTS:
                            copy_products()
                        if first and p:
                            finish[p - 1](g, NCH - 1)
                        elif not first:
                            finish[p](g, c - 1)
                sweep(act, chunk)
            for g in range(G):
                finish2(g, NCH - 1)

        @block.vector
        def _(dve):
            def set_up():
                dve.sem_inc(out_done, 16)
                nc.vector.memset(ones[:, :], 1.0).then_inc(biases, 1)
                dve.wait_ge(w_in, 16 * 12)
                dve.wait_ge(biases, 1)
                nc.vector.tensor_scalar(scale[:, :], scale[:, :], 1.0, 1.0, ALU.add, ALU.add)
                nc.vector.tensor_tensor(b_out1, b_out1, b_self1, ALU.add)
                nc.vector.tensor_tensor(out2_rows[:, D:DH], b_out2, b_self2, ALU.add)
                nc.vector.tensor_copy(ident_r[:, :], ident[:, :])
                nc.vector.tensor_copy(part0[:, 0:1], ident[:, 0:1])
                nc.vector.tensor_scalar(part0[:, 1:2], ident[:, 0:1], -1.0, 1.0, ALU.mult, ALU.add)
                nc.vector.tensor_scalar(rows01[:, :], ones[:, :], ident[:, 0:1], ident[:, 1:2], ALU.mult, ALU.add)
                for b in range(3):
                    last = nc.vector.tensor_scalar(col_rep[:, b, :], ident[:, :], 0.0, bias_cols[:, 10 + b:11 + b],
                                                   ALU.mult, ALU.add)
                last.then_inc(setup, 1)
                dve.wait_ge(setup, 1)

            def split(p, c, g, in_between=None):
                first = p == 0 and isinstance(c, int) and c == 0
                s = slot_of(p, c, g)
                src, low = raw[:, s, :], lo[:, g % NSPLIT, :]
                if first and g == 0:
                    low_features(dve, nc.vector, range(FIRST_X))
                if p == 0:
                    wait_ge(dve, raw_in[s], 16 * uses(p, c, g))
                    if not (first and g < NSPLIT):
                        wait_ge(dve, used, tile(p, c, g) - NSPLIT + 1)
                    nc.vector.scalar_tensor_tensor(low, src, SMALL, src, ALU.is_le, ALU.logical_and,
                                                   accum_out=small_n[:, ds(c * G + g, 1)]).then_inc(count_done, 1)
                    wait_ge(dve, count_done, c * G + g + 1)
                wait_ge(dve, hi_done, at(p, c, g) + 1)
                if in_between:
                    in_between()
                nc.vector.tensor_tensor(low, src, hi[:, g % NSPLIT, :].bitcast(f32), ALU.subtract)\
                    .then_inc(lo_done, 1)

            def mask(p, c, g, flag):
                n = c * G + ((p - 1) * TILES + g)
                src = raw[:, g % NRAW, :]
                with dve.If(flag == 1):
                    before = n * 3 if p == 1 else n + 2 * TILES
                    half = (c % 2) * CH
                    wait_ge(dve, rb_in, (c + ((p - 1) * NCH + 1)) * 16)
                    wait_ge(dve, raw_in[g % NRAW], 16 * uses(p, c, g))
                    for k in range(KT):
                        part = src[:, k * CH:(k + 1) * CH]
                        last = nc.vector.tensor_tensor(part, part, rb[:, ds(half, CH)], ALU.mult)
                    last.then_inc(gen, 1)
                    wait_ge(dve, gen, before + 1)
                    made = nc.vector.scalar_tensor_tensor(src, src, THRESH, src, ALU.is_gt, ALU.mult)
                    if p == 2:
                        made.then_inc(masked, 1)
                    else:
                        made.then_inc(gen, 1)
                        wait_ge(dve, gen, before + 2)
                        acc = w_acc[:, ds(half, CH)]
                        parts = [src[:, k * CH:(k + 1) * CH] for k in range(KT)]
                        if g == 0:
                            if not (isinstance(c, int) and c < 2):
                                wait_ge(dve, wsum_in, c - 1)
                            nc.vector.tensor_copy(acc, parts[0]).then_inc(gen, 1)
                        else:
                            wait_ge(dve, masked, n)
                            nc.vector.tensor_tensor(acc, acc, parts[0], ALU.add).then_inc(gen, 1)
                        wait_ge(dve, gen, before + 3)
                        nc.vector.tensor_tensor(acc, acc, parts[1], ALU.add).then_inc(masked, 1)
                with dve.Else():
                    dve.sem_inc(masked, 1)

            def layer_norm_stats(chain, y, width, tiles=range(TPC)):
                chain.wait()
                for t in tiles:
                    last = nc.vector.bn_stats(stats[:, t, :], y[:, t * width:(t + 1) * width])
                chain.step(last)

            def layer_norm_variance(chain, ready, tiles=range(TPC)):
                chain.wait()
                dve.sem_inc(passed, 1)
                for t in tiles:
                    last = nc.vector.bn_aggr(mv[:, t, :], stats[:, t, :])
                last.then_inc(ready, 1)

            def normalise(dst, y, width, tiles=slice(0, TPC)):
                for t in range(tiles.start, tiles.stop):
                    cols = slice(t * width, (t + 1) * width)
                    last = nc.vector.tensor_scalar(dst[:, cols], y[:, cols], mv[:, t, 0:1], rstd[:, t:t + 1],
                                                   ALU.subtract, ALU.mult)
                return last

            chains = {}

            def mean_shift():
                return nc.vector.scalar_tensor_tensor(shift[:, :], mv[:, :, 0], -1.0, rstd[:, :], ALU.mult, ALU.mult)

            def row4(row):
                return row.rearrange("p (a n) -> p a n", a=1).broadcast_to([128, TPC, row.shape[-1]])

            def t4(x):
                return x.rearrange("p (t n) -> p t n", t=TPC)

            def finish0(g, c):
                if g == V0_RES:
                    k = chains[0] = Chain(dve, v0, V0, c)
                    wait_ge(dve, x_lo_done, XT)
                    k.step(nc.vector.tensor_tensor(res0, xs_hi[:, 0, ds(c * CH, CH)].bitcast(f32),
                                                   xs_lo[:, 0, ds(c * CH, CH)].bitcast(f32), ALU.add))
                    k.wait()
                    k.step(nc.vector.tensor_tensor(t4(res0), t4(res0), row4(bm_row), ALU.add))
                k = chains.get(0)
                if g == V0_Y:
                    wait_ge(dve, merged, c + 1)
                    k.wait()
                    k.step(nc.vector.tensor_tensor(y0, sm[:, 2, :], res0, ALU.add))
                if g == V0_ST:
                    layer_norm_stats(k, y0, D)
                    layer_norm_variance(k, var0)
                if g == V0_NORM:
                    wait_ge(dve, inv0, c + 1)
                    normalise(y0, y0, D).then_inc(h_nat, 1)
                    assert k.n == V0, k.n
                if g == V0_H:
                    wait_ge(dve, h_hi_done, c + 1)
                    nc.vector.tensor_tensor(h_lo[:, ds(c * CH, CH)], y0, h_hi[:, ds(c * CH, CH)].bitcast(f32),
                                            ALU.subtract).then_inc(h_lo_done, 1)

            def node_factors(wsum, r, nodes, steps, before):
                rec, has, q, width = nd[:, 1], nd[:, 2], nd[:, 3], wsum.shape[-1]
                rec, has, q = (x[:, 0:width] for x in (rec, has, q))
                nc.vector.tensor_scalar(rec, wsum, EPS, None, ALU.add).then_inc(steps, 1)
                wait_ge(dve, steps, before + 1)
                nc.vector.tensor_scalar(has, wsum, 0.0, None, ALU.is_gt)
                nc.vector.reciprocal(rec, rec).then_inc(steps, 1)
                wait_ge(dve, steps, before + 2)
                nc.vector.tensor_tensor(q, rec, r, ALU.mult)
                nc.vector.tensor_tensor(rec, wsum, rec, ALU.mult)
                nc.vector.tensor_scalar(ne[:, nodes], has, -1.0, 1.0, ALU.mult, ALU.add).then_inc(steps, 1)
                wait_ge(dve, steps, before + 3)
                nc.vector.tensor_tensor(qe[:, nodes], q, has, ALU.mult)
                nc.vector.scalar_tensor_tensor(beta[:, nodes], rec, -1.0, ne[:, nodes], ALU.add, ALU.add)\
                    .then_inc(steps, 1)
                wait_ge(dve, steps, before + 4)

            def finish1(g, c, flag):
                if g == 0:
                    chains[0] = Chain(dve, v1, V1, c)
                    with dve.If(flag == 1):
                        wait_ge(dve, masked, (c + 1) * G)
                        nc.vector.tensor_copy(wk_sum, w_acc[:, ds((c % 2) * CH, CH)]).then_inc(wsum_in, 1)
                    with dve.Else():
                        dve.sem_inc(wsum_in, 1)
                    nc.vector.tensor_tensor(h_n, h_hi[:, ds(c * CH, CH)].bitcast(f32),
                                            h_lo[:, ds(c * CH, CH)].bitcast(f32), ALU.add).then_inc(hn_sb, 1)
                k = chains.get(0)
                if g == 3:
                    with dve.If(flag == 1):
                        wait_ge(dve, wsum_ps, c + 1)
                        nc.vector.tensor_copy(nd[:, 0, 0:TPC], sm[:, 3, 0:TPC]).then_inc(node_steps, 1)
                        wait_ge(dve, node_steps, c * 5 + 5)
                        node_factors(nd[:, 0, 0:TPC], ones[:, 0:TPC], ds(c * TPC, TPC), node_steps, c * 5 + 5)
                        nc.vector.tensor_copy(nd[:, 0, 0:1], ones[:, 0:1]).then_inc(node_v, 1)
                    with dve.Else():
                        dve.sem_inc(node_v, 1)
                if g in V_Y1:
                    half = V_Y1.index(g)
                    wait_ge(dve, o1_ps, c * 2 + half + 1)
                    wait_ge(dve, self_sb, c * 2 + half + 1)
                    tiles = range(2 * half, 2 * half + 2)
                    for t in tiles:
                        last = nc.vector.scalar_tensor_tensor(y1[:, t, :], sm[:, half, (t % 2) * DH:(t % 2 + 1) * DH],
                                                              qe[:, ds(c * TPC + t, 1)], y1[:, t, :],
                                                              ALU.mult, ALU.add)
                    k.step(last)
                    with dve.If(flag == 1):
                        wait_ge(dve, lone_ps, c + 1)
                        k.wait()
                        for t in tiles:
                            last = nc.vector.scalar_tensor_tensor(y1[:, t, :], bc1_row[:, :], beta[:, ds(c * TPC + t, 1)],
                                                                  y1[:, t, :], ALU.mult, ALU.add)
                        last.then_inc(lone_steps, 1)
                        wait_ge(dve, lone_steps, c * 4 + 2 * half + 1)
                        for t in tiles:
                            last = nc.vector.scalar_tensor_tensor(y1[:, t, :], pair[:, t, :], ne[:, ds(c * TPC + t, 1)],
                                                                  y1[:, t, :], ALU.mult, ALU.add)
                        last.then_inc(lone_steps, 1)
                        wait_ge(dve, lone_steps, c * 4 + 2 * half + 2)
                        nc.vector.tensor_copy(nd[:, 0, 0:1], ones[:, 0:1])
                    with dve.Else():
                        dve.sem_inc(passed, 1)
                for half in (h for h in range(2) if V_ST[h] == g):
                    layer_norm_stats(k, y1.rearrange("p t n -> p (t n)"), DH, range(2 * half, 2 * half + 2))
                for half in (h for h in range(2) if V_AGGR[h] == g):
                    layer_norm_variance(k, var1, range(2 * half, 2 * half + 2))
                if g in V_NORM:
                    half = V_NORM.index(g)
                    wait_ge(dve, inv1, c * 2 + half + 1)
                    flat = y1.rearrange("p t n -> p (t n)")
                    normalise(flat, flat, DH, slice(2 * half, 2 * half + 2)).then_inc(z_sb, 1)
                if g == V_G2:
                    assert k.n == V1, k.n
                    for half in range(2):
                        wait_ge(dve, g2_sb, c * 2 + half + 1)
                        g2 = sm[:, 2 + half, :].rearrange("p (b m n) -> p b m n", b=2, m=2)
                        for m, (up, low) in enumerate(((t_hi, t_lo), (own_hi, own_lo))):
                            cols = ds(c * CH + half * DH, DH)
                            last = nc.vector.tensor_tensor(low[:, cols].rearrange("p (t n) -> p t n", n=D), g2[:, :, m, :],
                                                           up[:, cols].bitcast(f32).rearrange("p (t n) -> p t n", n=D),
                                                           ALU.subtract)
                    last.then_inc(t_lo_done, 1)

            def finish2(g, c, flag):
                if g == V2_Y:
                    k = chains[0] = Chain(dve, v2, V2, c)
                    with dve.If(flag == 1):
                        wait_ge(dve, u_scaled, c + 1)
                        for n, part in enumerate((t_hi, t_lo)):
                            for t in range(TPC):
                                cols = slice(t * D, (t + 1) * D)
                                last = nc.vector.scalar_tensor_tensor(
                                    u_n[:, cols], part[:, ds(c * CH + t * D, D)].bitcast(f32),
                                    ne[:, ds(c * TPC + t, 1)], u_n[:, cols], ALU.mult, ALU.add)
                            last.then_inc(own_steps, 1)
                            wait_ge(dve, own_steps, c * 2 + n + 1)
                        nc.vector.tensor_copy(nd[:, 0, 0:1], ones[:, 0:1])
                    with dve.Else():
                        dve.sem_inc(passed, 1)
                    wait_ge(dve, u_scaled, c + 1)
                    wait_ge(dve, y2_ps, c + 1)
                    k.step(nc.vector.tensor_tensor(u_n, sm[:, 1, :], u_n, ALU.add))
                k = chains.get(0)
                if g == V2_ST:
                    layer_norm_stats(k, u_n, D)
                if g == V2_AGGR:
                    if not isinstance(c, int) or c:
                        wait_ge(dve, out_sb, c)
                    layer_norm_variance(k, var2)
                if g == V2_SHIFT:
                    wait_ge(dve, inv2, c * 2 + 1)
                    mean_shift().then_inc(rstd2, 1)
                if g == V2_GAMMA:
                    wait_ge(dve, z2_sb, c + 1)
                    k.step(nc.vector.tensor_tensor(t4(z2), t4(z2), row4(g2_row), ALU.mult))
                if g == V2_BETA:
                    k.wait()
                    k.step(nc.vector.tensor_tensor(t4(z2), t4(z2), row4(be2_row), ALU.add))
                if g == V2_RELU:
                    k.wait()
                    k.step(nc.vector.scalar_tensor_tensor(z2, z2, 0.0, sm[:, 2, :], ALU.max, ALU.add))
                if g == V2_ST2:
                    layer_norm_stats(k, z2, D)
                if g == V2_AGGR2:
                    layer_norm_variance(k, var2)
                if g == V2_OUT:
                    wait_ge(dve, inv2, c * 2 + 2)
                    mean_shift().then_inc(rstd2, 1)
                    assert k.n == V2, k.n

            def lay_out_biases():
                dve.wait_ge(prod_sb, 1)
                nc.vector.tensor_tensor(b_out1, b_out1, bc1_row[:, :], ALU.add).then_inc(biases, 1)
                dve.wait_ge(biases, 2)
                for n, (dst, row) in enumerate(((add1, b_out1), (add2, out2_rows))):
                    high, low = wk[:, 4, 0:DH], wk[:, 4, DH:2 * DH]
                    nc.vector.tensor_copy(dst[:, :], row).then_inc(biases, 1)
                    dve.wait_ge(biases, 4 * n + 3)
                    nc.vector.tensor_tensor(low, row, dst[:, :].bitcast(f32), ALU.subtract).then_inc(biases, 1)
                    dve.wait_ge(biases, 4 * n + 4)
                    nc.vector.tensor_scalar(low, low, part0[:, 1:2], None, ALU.mult).then_inc(biases, 1)
                    dve.wait_ge(biases, 4 * n + 5)
                    nc.vector.scalar_tensor_tensor(dst[:, :], dst[:, :].bitcast(f32), part0[:, 0:1], low,
                                                   ALU.mult, ALU.add).then_inc(biases, 1)
                dve.wait_ge(biases, 10)

            def column_sums():
                dve.wait_ge(hi_done, XT + TILES)
                dve.wait_ge(count_done, TILES)
                nc.vector.tensor_reduce(s_all[:, :], s_part[:, :].rearrange("p (k c) -> p k c", c=NCH),
                                        axis=AX.X, op=ALU.add).then_inc(totals, 1)
                dve.wait_ge(totals, 1)
                nc.vector.tensor_scalar(over[:, 0:TN], s_all[:, :], SUM_LIMIT, None, ALU.is_ge)
                nc.vector.tensor_scalar(over[:, TN:2 * TN], s_all[:, :], 0.0, None, ALU.is_le)
                nc.vector.tensor_scalar(r_all[:, :], s_all[:, :], EPS, None, ALU.add).then_inc(totals, 1)
                dve.wait_ge(totals, 2)
                nc.vector.reciprocal(r_all[:, :], r_all[:, :])
                nc.vector.tensor_reduce(small_n[:, TILES:TILES + 1], over[:, :], axis=AX.X, op=ALU.add)\
                    .then_inc(totals, 1)
                dve.wait_ge(totals, 3)
                nc.vector.tensor_reduce(bad[:, 0:1], small_n[:, :], axis=AX.X, op=ALU.add).then_inc(totals, 1)

            for g in range(G):
                split(0, 0, g)
                if g == V_SETUP:
                    set_up()
                if g == V_BIASES:
                    lay_out_biases()
            with dve.Fori(1, NCH - 1) as c:
                for g in range(G):
                    split(0, c, g)
                    finish0(g, c - 1)
            for g in range(G):
                split(0, NCH - 1, g, column_sums if g == G - 1 else None)
                finish0(g, NCH - 2)
            dve.wait_ge(flag_ps, 1)
            nc.vector.tensor_scalar(flag_i[:, :], sm[:, 3, 0:1], 0.0, None, ALU.is_gt)
            nc.vector.tensor_copy(r_rows[:, :], sm[0:TN, 3, 128:256]).then_inc(r_rows_sb, 1)
            dve.wait_ge(r_rows_sb, 1)
            nc.vector.tensor_tensor(ws_fast[:, :], s_all[:, :], r_all[:, :], ALU.mult).then_inc(flag_v, 1)
            dve.wait_ge(flag_v, 1)
            flag = dve.value_load(flag_i[0:1, 0:1], min_val=0, max_val=1)

            for g in range(LOOK):
                mask(1, 0, g, flag)
            for p in (1, 2):
                def chunk(c, p=p, last=False):
                    first = isinstance(c, int) and c == 0
                    for g in range(G):
                        if g + LOOK < G:
                            mask(p, c, g + LOOK, flag)
                        elif not last:
                            mask(p, c + 1, g + LOOK - G, flag)
                        elif p == 1:
                            mask(2, 0, g + LOOK - G, flag)
                        split(p, c, g)
                        if first and p == 1 and g == 1:
                            node_factors(ws_fast[:, :], r_all[:, :], slice(0, TN), node_steps, 0)
                        if first:
                            finish0(g, NCH - 1) if p == 1 else finish1(g, NCH - 1, flag)
                        else:
                            (finish1 if p == 1 else finish2)(g, c - 1, flag)
                chunk(0)
                with dve.Fori(1, NCH - 1) as c:
                    chunk(c)
                chunk(NCH - 1, last=True)
            for g in range(G):
                finish2(g, NCH - 1, flag)

        @block.tensor
        def _(pe):
            def weight_products():
                pe.wait_ge(w_in, 16 * 12)
                pe.wait_ge(setup, 1)
                w_in1t = axA[:, 0:DH].rearrange("p (a n) -> p a n", a=2)
                w_out1 = m1A.rearrange("p (a n) -> p a n", a=2)
                w_out2 = y0[:, 0:D]
                for a in range(2):
                    nc.tensor.matmul(sm[:, 0, 0:DH], w_in1t[:, a, :], w_out1[:, a, :], start=a == 0, stop=a == 1)
                for a in range(2):
                    nc.tensor.matmul(sm[:, 1, 0:DH], col_rep[:, a, :], w_out1[:, a, :], start=a == 0, stop=a == 1)
                for a in range(2):
                    nc.tensor.matmul(sm[:, 2, a * D:(a + 1) * D], w_in2t[:, a, :], w_out2, start=True, stop=True)
                nc.tensor.matmul(sm[:, 3, 0:D], col_rep[:, 2, :], w_out2, start=True, stop=True).then_inc(prod_ps, 1)

            def aggregate(p, c, g):
                feats = [(xs_hi[:, 0, :], xs_lo[:, 0, :]), (xs_hi[:, 1, :], xs_lo[:, 1, :])] if p == 0 \
                    else [(h_hi[:, :], h_lo[:, :])] if p == 1 else [(t_hi, t_lo)]
                if p == 0 and isinstance(c, int) and c == 0 and g % 4 == 0:
                    pe.wait_ge(x_lo_done, 2 * (g // 4 + 1))
                ts = [g * KT + k for k in range(KT)]
                if p and isinstance(c, int) and ts[0] in (0, TPC * (NCH - 1)):
                    pe.wait_ge(h_lo_done if p == 1 else t_lo_done, NCH if g else NCH - 1)
                slot = g % NSPLIT
                wait_ge(pe, hi_done, at(p, c, g) + 1)
                last = None

                def product(f, weights, moving, t, k, first, final):
                    bank = (c % 2) * CH + f * 2 * CH
                    return nc.tensor.matmul(big[:, ds(bank, CH)], weights[:, t * D:(t + 1) * D],
                                            moving[:, slot, k * CH:(k + 1) * CH], start=first, stop=final)
                for k, t in enumerate(ts):
                    for f, (w_hi, w_lo) in enumerate(feats):
                        product(f, w_hi, hi, t, k, g == 0 and k == 0, False)
                        product(f, w_lo, hi, t, k, False, False)
                wait_ge(pe, lo_done, tile(p, c, g) + 1)
                for k, t in enumerate(ts):
                    for f, (w_hi, w_lo) in enumerate(feats):
                        last = product(f, w_hi, lo, t, k, False, g == G - 1 and k == KT - 1)
                last.then_inc(used, 1)

            def finish0(g, c):
                if g in P0_MLP:
                    layer = P0_MLP.index(g)
                    if layer == 0:
                        wait_ge(pe, agg_out, c + 1)
                    else:
                        wait_ge(pe, mlp_sb, c * LAYERS + layer)
                    src = ((axA, axB), (m1A, m1B))[layer % 2]
                    for b in range(2):
                        last = nc.tensor.matmul(sm[:, b, :], mlp[:, b * LAYERS + layer, :], src[b],
                                                start=True, stop=True)
                    last.then_inc(mlp_ps, 1)
                if g == P0_MERGE:
                    wait_ge(pe, mlp_sb, c * LAYERS + LAYERS)
                    for t in range(TPC):
                        for b, src in enumerate((m1A, m1B)):
                            last = nc.tensor.matmul(sm[:, 2, t * D:(t + 1) * D], src[:, t * D:(t + 1) * D],
                                                    merge[:, b, :], start=b == 0, stop=b == 1)
                    last.then_inc(merged, 1)

            def finish1(g, c, flag):
                if g == 0:
                    wait_ge(pe, wsum_in, c + 1)
                    with pe.If(flag == 1):
                        for t in range(TPC):
                            last = nc.tensor.matmul(sm[:, 3, t:t + 1], wk_sum[:, t * D:(t + 1) * D], ones[:, 0:1],
                                                    start=True, stop=True)
                        last.then_inc(wsum_ps, 1)
                    with pe.Else():
                        pe.sem_inc(wsum_ps, 1)
                if g == P_HT:
                    wait_ge(pe, hn_sb, c + 1)
                    for t in range(TPC):
                        last = nc.tensor.transpose(sm[:, 2, t * D:(t + 1) * D], h_n[:, t * D:(t + 1) * D], ident[:, :])
                    last.then_inc(ht_ps, 1)
                if g in P_SELF:
                    half = P_SELF.index(g)
                    wait_ge(pe, ht_sb, c + 1)
                    for t in range(2 * half, 2 * half + 2):
                        nc.tensor.matmul(pair[:, t, :], rows01[:, :], add1[:, :], start=True, stop=False)
                        last = nc.tensor.matmul(pair[:, t, :], h_t[:, t * D:(t + 1) * D], w_self1[:, :],
                                                start=False, stop=True)
                    last.then_inc(self_ps, 1)
                if g in P_OUT:
                    half = P_OUT.index(g)
                    wait_ge(pe, agg_out, c + NCH + 1)
                    for t in range(2 * half, 2 * half + 2):
                        last = nc.tensor.matmul(sm[:, half, (t % 2) * DH:(t % 2 + 1) * DH], ut[:, t * D:(t + 1) * D],
                                                w_c1[:, :], start=True, stop=True)
                    last.then_inc(o1_ps, 1)
                if g == P_LONE:
                    with pe.If(flag == 1):
                        wait_ge(pe, self_sb, c * 2 + 2)
                        for t in range(TPC):
                            last = nc.tensor.matmul(pair[:, t, :], h_t[:, t * D:(t + 1) * D], w_c1[:, :],
                                                    start=True, stop=True)
                        last.then_inc(lone_ps, 1)
                    with pe.Else():
                        pe.sem_inc(lone_ps, 1)
                if g in P_Z:
                    half = P_Z.index(g)
                    wait_ge(pe, z_sb, c * 2 + half + 1)
                    for b in range(2):
                        for t in range(2):
                            last = nc.tensor.transpose(sm[:, half, b * DH + t * D:b * DH + (t + 1) * D],
                                                       y1[:, 2 * half + t, b * D:(b + 1) * D], ident[:, :])
                    last.then_inc(z_ps, 1)
                if g in P_G2:
                    half = P_G2.index(g)
                    wait_ge(pe, h2_sb, c * 2 + half + 1)
                    for t in range(2 * half, 2 * half + 2):
                        dst = sm[:, 2 + half, (t % 2) * DH:(t % 2 + 1) * DH]
                        nc.tensor.matmul(dst, rows01[:, :], add2[:, :], start=True, stop=False)
                        for b in range(2):
                            last = nc.tensor.matmul(dst, h2t[:, b, t * D:(t + 1) * D],
                                                    w_2[:, b, :, :].rearrange("p a n -> p (a n)"),
                                                    start=False, stop=b == 1)
                    last.then_inc(g2_ps, 1)

            def finish2(g, c):
                if g == P2_T:
                    wait_ge(pe, agg_out, c + 2 * NCH + 1)
                    for t in range(TPC):
                        last = nc.tensor.transpose(sm[:, 0, t * D:(t + 1) * D], ut[:, t * D:(t + 1) * D], ident[:, :])
                    last.then_inc(t_ps, 1)
                if g == P2_Y:
                    wait_ge(pe, t_lo_done, c + 1)
                    for bank, parts in ((1, (own_hi, own_lo)), (2, (h_hi, h_lo))):
                        for n, part in enumerate(parts):
                            last = nc.tensor.matmul(sm[:, bank, :], ident_r[:, :], part[:, ds(c * CH, CH)],
                                                    start=n == 0, stop=n == 1)
                    last.then_inc(y2_ps, 1)

            flag = None
            for p in range(3):
                def chunk(c, p=p):
                    first = isinstance(c, int)
                    for g in range(G):
                        aggregate(p, c, g)
                        if first:
                            if p == 0 and g == P_PRODUCTS:
                                weight_products()
                            if p == 1:
                                finish0(g, NCH - 1)
                            if p == 2:
                                finish1(g, NCH - 1, flag)
                        elif p == 0:
                            finish0(g, c - 1)
                        elif p == 1:
                            finish1(g, c - 1, flag)
                        else:
                            finish2(g, c - 1)
                if p:
                    sweep(pe, chunk)
                else:
                    chunk(0)
                    with pe.Fori(1, NCH - 1) as c:
                        chunk(c)
                    for g in range(G):
                        if g == G - 1:
                            pe.wait_ge(totals, 4)
                            nc.tensor.matmul(sm[:, 3, 0:1], ones[:, :], bad[:, 0:1], start=True, stop=True)
                            nc.tensor.transpose(sm[0:TN, 3, 128:256], r_all[:, :], ident[:, :]).then_inc(flag_ps, 1)
                        aggregate(0, NCH - 1, g)
                        finish0(g, NCH - 2)
                    pe.wait_ge(flag_v, 1)
                    flag = pe.value_load(flag_i[0:1, 0:1], min_val=0, max_val=1)
            for g in range(G):
                finish2(g, NCH - 1)


def kernel(**inputs):
    import concourse.bacc as _bacc
    from concourse.bass_utils import run_bass_kernel_spmd as _run

    a = {k: np.asarray(v) for k, v in inputs.items()}
    adj = a["adj"]

    def blocks(m):
        return np.ascontiguousarray(
            m.reshape(G, KT, 128, NCH, CH).transpose(3, 0, 2, 1, 4)).reshape(NCH * G, 128, LOAD)

    def nodes(x):
        return np.ascontiguousarray(x.reshape(TN, 128, D).transpose(1, 0, 2)).reshape(128, N)

    def halves(w):
        return np.ascontiguousarray(w.reshape(2, 128, -1).transpose(1, 0, 2))

    p0, p1 = "L0_gnn_", "L1_gnn_"
    mlp_w = np.stack([w for b in ("W1", "W2") for w in a[p0 + b]]).transpose(2, 0, 1)
    merge_w = halves(a[p0 + "Wm"].T)
    cols = np.concatenate([
        a[p0 + "b1"].T, a[p0 + "b2"].T, a[p1 + "g1"].reshape(2, 128).T, a[p1 + "be1"].reshape(2, 128).T,
        a[p1 + "b_in1"].reshape(2, 128).T, a[p1 + "b_in2"].reshape(128, 1)], axis=1)
    rows = np.concatenate([a[p0 + "bm"], a[p1 + "g2"], a[p1 + "be2"], a[p1 + "b_out2"], a[p1 + "b_self2"],
                           np.zeros(2 * D, np.float32), a[p1 + "b_out1"], a[p1 + "b_self1"]])
    arrays = {
        "adj_rows": blocks(adj.T), "adj_cols": blocks(adj), "x_in": nodes(a["x"]), "x2_in": nodes(a[p0 + "x2"]),
        "mlp_w": mlp_w, "merge_w": merge_w, "win1_t": halves(a[p1 + "W_in1"].T).reshape(128, DH),
        "wout1": halves(a[p1 + "W_out1"]).reshape(128, 512), "wself1": a[p1 + "W_self1"],
        "win2_t": a[p1 + "W_in2"].T.reshape(128, 2, 128), "wout2": a[p1 + "W_out2"], "wself2": halves(a[p1 + "W_self2"]),
        "cols_in": cols, "rows_in": rows, "eps_in": np.concatenate([a[p0 + "eps1"], a[p0 + "eps2"]]),
        "ident_in": np.eye(128, dtype=np.float32),
    }
    arrays = {k: np.ascontiguousarray(v) for k, v in arrays.items()}
    nc = _bacc.Bacc("TRN2", target_bir_lowering=False, num_devices=1, dynamic_dma_scratch_size=8192)
    f32 = mybir.dt.float32
    args = {k: nc.dram_tensor(k, v.shape, f32, kind="ExternalInput").ap() for k, v in arrays.items()}
    args["r_dram"] = nc.dram_tensor("r_dram", (TN, 128), f32).ap()
    args["out"] = nc.dram_tensor("out", (NCH, 128, CH), f32, kind="ExternalOutput").ap()
    gnn_kernel(nc, **args)
    r = _run(nc, [arrays], core_ids=[0])
    got = np.asarray(r.results[0]["out"])
    return np.ascontiguousarray(got.reshape(NCH, 128, TPC, 128).transpose(0, 2, 1, 3)).reshape(N, D)
```
